# Optimizing a Trainium2 kernel written in Bass

```python
import numpy as np
import jax
import jax.numpy as jnp

def _softmax(x, axis=-1):
    return jax.nn.softmax(x, axis=axis)

def _gelu(x):
    return jax.nn.gelu(x, approximate=True)

def _silu(x):
    return jax.nn.silu(x)

def _sigmoid(x):
    return jax.nn.sigmoid(x)

def _layernorm(x, axis=-1, eps=1e-05):
    m = jnp.mean(x, axis=axis, keepdims=True)
    v = jnp.var(x, axis=axis, keepdims=True)
    return (x - m) / jnp.sqrt(v + eps)

def _scatter_add(tgt, idx, src, axis=0):
    return tgt.at[idx].add(src)

def _segment_sum(src, seg, n):
    return jax.ops.segment_sum(src, seg, n)
kernel_name = 'mk_metaformer_d1_conv_nchw256_r4_8d0fac'

def setup_inputs(seed: int=0):
    np.random.seed(seed)
    _w = jnp.asarray

    def _rec_inputs():
        import jax
        import jax.numpy as jnp
        _gk = jax.random.key(seed)
        x = -0.0002928 + 1 * jax.random.normal(jax.random.fold_in(_gk, 1), (4, 64, 16, 16), jnp.float32)
        return x
    x = _rec_inputs()

    def _L0_conv_setup():
        import jax, jax.numpy as jnp
        import numpy as np
        K_SIZE = 3
        STRIDE = 1
        DIL = 1
        PAD = (K_SIZE - 1) // 2 * DIL
        OFF_PAD = (K_SIZE - 1) // 2
        KK = K_SIZE * K_SIZE

        def _bilinear_sample(x, ys, xs):
            B, C, H, W = x.shape
            _, K, Ho, Wo = ys.shape
            y0 = jnp.floor(ys)
            x0 = jnp.floor(xs)
            y1, x1 = (y0 + 1.0, x0 + 1.0)
            wy1 = ys - y0
            wy0 = 1.0 - wy1
            wx1 = xs - x0
            wx0 = 1.0 - wx1
            x_flat = x.reshape(B, C, H * W)

            def gather_term(yi, xi, wt):
                valid = (yi >= 0) & (yi < H) & (xi >= 0) & (xi < W)
                yc = jnp.clip(yi, 0, H - 1).astype(jnp.int32)
                xc = jnp.clip(xi, 0, W - 1).astype(jnp.int32)
                idx = (yc * W + xc).reshape(B, -1)
                g = jax.vmap(lambda xf, i: xf[:, i])(x_flat, idx)
                w = (wt * valid.astype(wt.dtype)).reshape(B, 1, -1)
                return g * w
            out = gather_term(y0, x0, wy0 * wx0) + gather_term(y0, x1, wy0 * wx1) + gather_term(y1, x0, wy1 * wx0) + gather_term(y1, x1, wy1 * wx1)
            return out.reshape(B, C, K, Ho, Wo)

        def _dcn_v2(x, w_off, b_off, w_dcn):
            B, C, H, W = x.shape
            om = jax.lax.conv_general_dilated(x, w_off, (STRIDE, STRIDE), [(OFF_PAD, OFF_PAD)] * 2, dimension_numbers=('NCHW', 'OIHW', 'NCHW')) + b_off[None, :, None, None]
            offset = om[:, :2 * KK]
            mask = jax.nn.sigmoid(om[:, 2 * KK:])
            Ho, Wo = (offset.shape[2], offset.shape[3])
            off = offset.reshape(B, KK, 2, Ho, Wo)
            off_y, off_x = (off[:, :, 0], off[:, :, 1])
            kh = (jnp.arange(KK) // K_SIZE).astype(jnp.float32)
            kw = (jnp.arange(KK) % K_SIZE).astype(jnp.float32)
            py = (jnp.arange(Ho) * STRIDE - PAD).astype(jnp.float32)
            px = (jnp.arange(Wo) * STRIDE - PAD).astype(jnp.float32)
            ys = py[None, None, :, None] + (kh * DIL)[None, :, None, None] + off_y
            xs = px[None, None, None, :] + (kw * DIL)[None, :, None, None] + off_x
            sampled = _bilinear_sample(x, ys, xs)
            sampled = sampled * mask[:, None]
            w = w_dcn.reshape(w_dcn.shape[0], C, KK)
            return jnp.einsum('bckhw,ock->bohw', sampled, w)
        key = jax.random.key(seed)
        k1, k2, k3, k4 = jax.random.split(key, 4)
        B, C, H, W = (4, 64, 16, 16)
        O = 64
        x = jax.random.normal(k1, (B, C, H, W), jnp.float32)
        w_off = jax.random.normal(k2, (3 * KK, C, K_SIZE, K_SIZE), jnp.float32) * 0.01
        b_off = jax.random.normal(k3, (3 * KK,), jnp.float32) * 0.01
        w_dcn = jax.random.normal(k4, (O, C, K_SIZE, K_SIZE), jnp.float32) * (1.0 / np.sqrt(C * KK))
        return {'x': x, 'w_off': w_off, 'b_off': b_off, 'w_dcn': w_dcn}
    _L0_conv_all = _L0_conv_setup()
    _L0_conv_in = {k: v for k, v in _L0_conv_all.items() if k in ('w_off', 'b_off', 'w_dcn')}
    del _L0_conv_all

    def _L0_ffn_setup():
        import jax, jax.numpy as jnp
        import numpy as np
        TOP_K = 2
        key = jax.random.key(seed)
        ks = jax.random.split(key, 4)
        B, L, D, H, E = (8, 1024, 64, 256, 8)
        s = 0.02
        return {'x': jax.random.normal(ks[0], (B, L, D), jnp.float32), 'Wg': jax.random.normal(ks[1], (D, E), jnp.float32) * s, 'bg': jnp.zeros((E,), jnp.float32), 'W1': jax.random.normal(ks[2], (E, D, H), jnp.float32) * s, 'b1': jnp.zeros((E, H), jnp.float32), 'W2': jax.random.normal(ks[3], (E, H, D), jnp.float32) * s, 'b2': jnp.zeros((E, D), jnp.float32)}
    _L0_ffn_all = _L0_ffn_setup()
    _L0_ffn_in = {k: v for k, v in _L0_ffn_all.items() if k in ('Wg', 'bg', 'W1', 'b1', 'W2', 'b2')}
    del _L0_ffn_all
    return {'x': x, 'L0_conv_w_off': _L0_conv_in['w_off'], 'L0_conv_b_off': _L0_conv_in['b_off'], 'L0_conv_w_dcn': _L0_conv_in['w_dcn'], 'L0_ffn_Wg': _L0_ffn_in['Wg'], 'L0_ffn_bg': _L0_ffn_in['bg'], 'L0_ffn_W1': _L0_ffn_in['W1'], 'L0_ffn_b1': _L0_ffn_in['b1'], 'L0_ffn_W2': _L0_ffn_in['W2'], 'L0_ffn_b2': _L0_ffn_in['b2']}

def reference(x, L0_conv_w_off, L0_conv_b_off, L0_conv_w_dcn, L0_ffn_Wg, L0_ffn_bg, L0_ffn_W1, L0_ffn_b1, L0_ffn_W2, L0_ffn_b2):
    import jax
    import jax.numpy as jnp

    def _L0_conv_ref(x, w_off, b_off, w_dcn):
        import jax, jax.numpy as jnp
        import numpy as np
        K_SIZE = 3
        STRIDE = 1
        DIL = 1
        PAD = (K_SIZE - 1) // 2 * DIL
        OFF_PAD = (K_SIZE - 1) // 2
        KK = K_SIZE * K_SIZE

        def _bilinear_sample(x, ys, xs):
            B, C, H, W = x.shape
            _, K, Ho, Wo = ys.shape
            y0 = jnp.floor(ys)
            x0 = jnp.floor(xs)
            y1, x1 = (y0 + 1.0, x0 + 1.0)
            wy1 = ys - y0
            wy0 = 1.0 - wy1
            wx1 = xs - x0
            wx0 = 1.0 - wx1
            x_flat = x.reshape(B, C, H * W)

            def gather_term(yi, xi, wt):
                valid = (yi >= 0) & (yi < H) & (xi >= 0) & (xi < W)
                yc = jnp.clip(yi, 0, H - 1).astype(jnp.int32)
                xc = jnp.clip(xi, 0, W - 1).astype(jnp.int32)
                idx = (yc * W + xc).reshape(B, -1)
                g = jax.vmap(lambda xf, i: xf[:, i])(x_flat, idx)
                w = (wt * valid.astype(wt.dtype)).reshape(B, 1, -1)
                return g * w
            out = gather_term(y0, x0, wy0 * wx0) + gather_term(y0, x1, wy0 * wx1) + gather_term(y1, x0, wy1 * wx0) + gather_term(y1, x1, wy1 * wx1)
            return out.reshape(B, C, K, Ho, Wo)

        def _dcn_v2(x, w_off, b_off, w_dcn):
            B, C, H, W = x.shape
            om = jax.lax.conv_general_dilated(x, w_off, (STRIDE, STRIDE), [(OFF_PAD, OFF_PAD)] * 2, dimension_numbers=('NCHW', 'OIHW', 'NCHW')) + b_off[None, :, None, None]
            offset = om[:, :2 * KK]
            mask = jax.nn.sigmoid(om[:, 2 * KK:])
            Ho, Wo = (offset.shape[2], offset.shape[3])
            off = offset.reshape(B, KK, 2, Ho, Wo)
            off_y, off_x = (off[:, :, 0], off[:, :, 1])
            kh = (jnp.arange(KK) // K_SIZE).astype(jnp.float32)
            kw = (jnp.arange(KK) % K_SIZE).astype(jnp.float32)
            py = (jnp.arange(Ho) * STRIDE - PAD).astype(jnp.float32)
            px = (jnp.arange(Wo) * STRIDE - PAD).astype(jnp.float32)
            ys = py[None, None, :, None] + (kh * DIL)[None, :, None, None] + off_y
            xs = px[None, None, None, :] + (kw * DIL)[None, :, None, None] + off_x
            sampled = _bilinear_sample(x, ys, xs)
            sampled = sampled * mask[:, None]
            w = w_dcn.reshape(w_dcn.shape[0], C, KK)
            return jnp.einsum('bckhw,ock->bohw', sampled, w)
        return _dcn_v2(x, w_off, b_off, w_dcn)

    def _L0_ffn_ref(x, Wg, bg, W1, b1, W2, b2):
        import jax, jax.numpy as jnp
        import numpy as np
        TOP_K = 2
        B, L, D = x.shape
        E = W1.shape[0]
        xf = x.reshape(-1, D)
        gate_logits = xf @ Wg + bg
        top_w, top_i = jax.lax.top_k(gate_logits, TOP_K)
        top_w = jax.nn.softmax(top_w, axis=-1)
        w_dense = jnp.sum(jax.nn.one_hot(top_i, E, dtype=xf.dtype) * top_w[..., None], axis=1)
        out = jnp.zeros_like(xf)
        for e in range(E):
            h = jax.nn.gelu(xf @ W1[e] + b1[e], approximate=False)
            out = out + w_dense[:, e:e + 1] * (h @ W2[e] + b2[e])
        return out.reshape(B, L, D)

    def _gn(v, G=32, eps=1e-05):
        B_, C_, H_, W_ = v.shape
        g = v.reshape(B_, G, C_ // G, H_, W_)
        m = jnp.mean(g, axis=(2, 3, 4), keepdims=True)
        s = jnp.var(g, axis=(2, 3, 4), keepdims=True)
        return ((g - m) / jnp.sqrt(s + eps)).reshape(v.shape)

    def _ln_c(v, eps=1e-06):
        m = jnp.mean(v, axis=1, keepdims=True)
        s = jnp.var(v, axis=1, keepdims=True)
        return (v - m) / jnp.sqrt(s + eps)

    def _ln_t(v, eps=1e-05):
        m = jnp.mean(v, axis=-1, keepdims=True)
        s = jnp.var(v, axis=-1, keepdims=True)
        return (v - m) / jnp.sqrt(s + eps)

    def _to_tokens(v):
        B_, C_, H_, W_ = v.shape
        return v.reshape(B_, C_, H_ * W_).transpose(0, 2, 1)

    def _from_tokens(t, like):
        B_, C_, H_, W_ = like.shape
        return t.transpose(0, 2, 1).reshape(B_, C_, H_, W_)
    x = x + _L0_conv_ref(_ln_c(x), L0_conv_w_off, L0_conv_b_off, L0_conv_w_dcn)
    t = _to_tokens(x)
    t = t + _L0_ffn_ref(_ln_t(t), L0_ffn_Wg, L0_ffn_bg, L0_ffn_W1, L0_ffn_b1, L0_ffn_W2, L0_ffn_b2)
    x = _from_tokens(t, x)
    return x

_drawn_inputs = setup_inputs


def setup_inputs(seed=0):
    import zlib

    import numpy as np

    out = dict(_drawn_inputs(seed))
    spreads = {'L0_ffn_bg': (0.0, 0.1), 'L0_ffn_b1': (0.0, 0.711), 'L0_ffn_b2': (0.0, 0.1)}
    factors = {'L0_conv_b_off': 8.0, 'L0_ffn_W1': 3.224, 'L0_ffn_W2': 2.67}
    for name, (base, spread) in spreads.items():
        noise = np.random.default_rng([zlib.crc32(name.encode()), seed]).standard_normal(out[name].shape)
        drawn = base * np.exp(spread * noise) if base else spread * noise
        out[name] = jnp.asarray(drawn.astype(out[name].dtype))
    for name, factor in factors.items():
        out[name] = (out[name] * factor).astype(out[name].dtype)
    return out
```

```python
from contextlib import ExitStack

import concourse.bass as bass
from concourse import mybir

F32 = mybir.dt.float32
F32R = mybir.dt.float32r
I32 = mybir.dt.int32
U32 = mybir.dt.uint32
ACT = mybir.ActivationFunctionType
ALU = mybir.AluOpType

P = 128
NB, C, H, W = 4, 64, 16, 16
HW = H * W
NT = HW // P
KS = 3
TAPS = KS * KS
OM = 3 * TAPS
O = 64
E, HID = 8, 256
HC = HID // P
PAIRS = E // 2
ST = HW // P
RPT = P // W
HP, WP = H + 2, W + 2
GROUP = 3
UNITS = TAPS // GROUP
SLOTS = NB * TAPS
STEPS = E * HC
CHAIN = 4
TAIL = 9
V_PIECES = [(st, lo, n) for st in range(ST) for lo, n in ((0, 5), (5, 4))]
LN_C_EPS, LN_T_EPS = 1e-6, 1e-5
AT_RING, A_RING, H_RING, TMP_RING = 3, 3, 3, 4


def tasks(slot):
    b, k = divmod(slot, TAPS)
    found = []
    n, after = b + 1, b - 1
    if n < NB:
        found += {0: [("conv", n)], 1: [("offsets", n)], 2: [("mask", n)]}.get(k, [])
        if 3 <= k < 3 + len(V_PIECES):
            found.append(("value", n, k - 3))
    if 0 <= after < NB:
        found += {0: [("residual", after)], 1: [("stats", after)], 2: [("norm", after)],
                  3: [("stack", after)], 4: [("gate", after)], 5: [("top", after)],
                  6: [("weights", after)], 7: [("spread", after, 0)],
                  8: [("spread", after, 1)]}.get(k, [])
    return found


def ffn_steps(slot):
    b, k = divmod(slot - TAPS - CHAIN, TAPS)
    if b < 0 or b >= NB:
        return []
    if b == NB - 1:
        ends = [0, 2, 4, 5, 8, STEPS]
        return [(b, i) for i in range(ends[k], ends[k + 1])] if k < len(ends) - 1 else []
    return [(b, i) for i in range(STEPS * k // TAPS, STEPS * (k + 1) // TAPS)]


LAST_SLOT = NB * TAPS + TAPS


def metaformer_kernel(nc, x_tok, x_ch, w_off, b_off, w_dcn, wg, bg, w1, b1, w2, b2, out):
    ctx = ExitStack()
    with ctx:
        def sb(name, shape, dt=F32):
            return ctx.enter_context(nc.sbuf_tensor(name, shape, dt))

        def ps(name):
            return ctx.enter_context(nc.psum_tensor(name, [P, 512], F32))

        def sem(name):
            return ctx.enter_context(nc.semaphore(name))

        xt = sb("xt", [P, NB * NT, C])
        xc = sb("xc", [C, NB, HW])
        woff_raw = sb("woff_raw", [P, TAPS, OM])
        wdcn_raw = sb("wdcn_raw", [P, TAPS, O])
        w1_raw = sb("w1_raw", [P, E, HID])
        wg_raw = sb("wg_raw", [P, E])
        boff_bc = sb("boff_bc", [P, OM])
        bg_bc = sb("bg_bc", [P, E])
        b1_col = sb("b1_col", [P, STEPS])
        b2_col = sb("b2_col", [P, PAIRS])
        w2_sb = sb("w2_sb", [P, E, HC, O])
        woff = sb("woff", [P, TAPS, 2 * OM], F32R)
        wdcn_hi = sb("wdcn_hi", [P, TAPS, O], F32R)
        wdcn_lo = sb("wdcn_lo", [P, TAPS, O], F32R)
        w1_hi = sb("w1_hi", [P, E, HID], F32R)
        w1_lo = sb("w1_lo", [P, E, HID], F32R)
        wg_hl = sb("wg_hl", [P, 2 * E], F32R)
        ident = sb("ident", [P, P])
        fold = sb("fold", [P, O])
        sel_f = sb("sel_f", [2 * E, PAIRS, 2, O])
        sel = sb("sel", [2 * E, PAIRS, 2 * O], F32R)
        grid = sb("grid", [P, W])
        eight = sb("eight", [P, E])
        power = sb("power", [P, NB * NT])
        pidx = sb("pidx", [P, 1], I32)
        prow_i = sb("prow_i", [P, 1], I32)
        pcol_i = sb("pcol_i", [P, 1], I32)
        prow = sb("prow", [P, 1])
        pcol = sb("pcol", [P, 1])
        tapyx = sb("tapyx", [P, 2 * TAPS])
        base = sb("base", [P, NT, OM])
        st1 = sb("st1", [P, NB * NT, 6])
        mv1 = sb("mv1", [P, NB * NT, 2])
        ve1 = sb("ve1", [P, NB * NT])
        rs1 = sb("rs1", [P, NB * NT])
        xn1 = sb("xn1", [P, NB * NT, C])
        xn1_hl = sb("xn1_hl", [P, NB * NT, 2 * C], F32R)
        xpad = sb("xpad", [P, NB, HP, WP], F32R)
        xflat = sb("xflat", [P, NB, HW], F32R)
        om_sb = sb("om_sb", [2 * OM, 2, HW])
        pos_a = sb("pos_a", [P, NT, OM])
        pos = sb("pos", [P, 2, NT, OM])
        tanh_m = sb("tanh_m", [P, 2, NT, TAPS])
        mask = sb("mask", [P, 2, NT, TAPS])
        dist = sb("dist", [P, NT, 2 * TAPS, W])
        adist = sb("adist", [P, NT, 2 * TAPS, W])
        hats = sb("hats", [P, 2, NT, 2 * TAPS, W])
        haty = sb("haty", [P, 2, NT, TAPS, W])
        at = sb("at", [P, AT_RING, NT, GROUP, HW])
        a_hi = sb("a_hi", [P, A_RING, ST, HW], F32R)
        a_lo = sb("a_lo", [P, A_RING, ST, HW], F32R)
        v_hl = sb("v_hl", [P, NB, ST, TAPS, 2 * O], F32R)
        c1 = sb("c1", [O, 2, HW])
        c2 = sb("c2", [O, 2, HW])
        t1 = sb("t1", [O, NB, HW])
        st2 = sb("st2", [P, NT, 6])
        mv2 = sb("mv2", [P, 2, NT, 2])
        ve2 = sb("ve2", [P, 2, NT])
        rs2 = sb("rs2", [P, 2, NT])
        xn2 = sb("xn2", [P, NT, C])
        xn2_hl = sb("xn2_hl", [P, NT, 2 * C], F32R)
        x2s = sb("x2s", [P, 2, HW], F32R)
        lg_sb = sb("lg_sb", [2 * E, HW])
        lg_a = sb("lg_a", [P, NT, E])
        logit = sb("logit", [P, NT, E])
        top = sb("top", [P, NT, 8])
        topi = sb("topi", [P, NT, 8], U32)
        topf = sb("topf", [P, NT, 2])
        diff = sb("diff", [P, NT])
        tanh_d = sb("tanh_d", [P, NT])
        pw = sb("pw", [P, NT, 2])
        onehot = sb("onehot", [P, NT, 2, E])
        gated = sb("gated", [P, NT, 2, E])
        wd = sb("wd", [P, NT, E])
        wd_hl = sb("wd_hl", [P, NT, 2 * E], F32R)
        wt = sb("wt", [2 * E, HW], F32R)
        spread = sb("spread", [P, 2, PAIRS, HW])
        hid = sb("hid", [P, H_RING, HW])
        tmp = sb("tmp", [P, TMP_RING, HW])
        ya = sb("ya", [P, 3, HW])
        fin = sb("fin", [O, NB, HW])

        bank_t = [ps("bank_t0"), ps("bank_t1")]
        bank_o = ps("bank_o")
        bank_p = ps("bank_p")
        bank_c = ps("bank_c")
        bank_h = [ps("bank_h0"), ps("bank_h1")]
        bank_y = ps("bank_y")
        V0_BANKS = [bank_c, bank_y, bank_o, bank_h[1]]

        ld_xt0, ld_xt1, ld_xc, ld_woff, ld_wdcn = (sem(n) for n in ("ld_xt0", "ld_xt1", "ld_xc", "ld_woff", "ld_wdcn"))
        ld_w1, ld_w2, ld_wg, ld_boff, ld_bias = (sem(n) for n in ("ld_w1", "ld_w2", "ld_wg", "ld_boff", "ld_bias"))
        pool_const = sem("pool_const")
        base_ready, woff_ready, wdcn_ready, wg_ready, w1_ready, fold_ready, sel_ready = (
            sem(n) for n in ("base_ready", "woff_ready", "wdcn_ready", "wg_ready", "w1_ready", "fold_ready", "sel_ready"))
        dve_chain, act_chain, pool_chain = sem("dve_chain"), sem("act_chain"), sem("pool_chain")
        var1, rstd1, xn1_ready, xn1T, xpad_ready, xflat_ready = (
            sem(n) for n in ("var1", "rstd1", "xn1_ready", "xn1T", "xpad_ready", "xflat_ready"))
        om_done, om_saved, omT, pos_ready, tanh_done, dist_ready, hats_ready, haty_ready = (
            sem(n) for n in ("om_done", "om_saved", "omT", "pos_ready", "tanh_done", "dist_ready", "hats_ready", "haty_ready"))
        v_done, v_hi, v_lo = sem("v_done"), sem("v_hi"), sem("v_lo")
        at_dve, at_pool = sem("at_dve"), sem("at_pool")
        tap_T, tap_hi, tap_lo, tap_mm = sem("tap_T"), sem("tap_hi"), sem("tap_lo"), sem("tap_mm")
        lo_half, t1_ready, t1T, var2, rstd2, xn2_ready, xn2T, x2s_ready = (
            sem(n) for n in ("lo_half", "t1_ready", "t1T", "var2", "rstd2", "xn2_ready", "xn2T", "x2s_ready"))
        lg_done, lg_saved, lgT, diff_ready, tanh_d_done, wd_ready, wdT, wt_ready, spread_done, spread_ready = (
            sem(n) for n in ("lg_done", "lg_saved", "lgT", "diff_ready", "tanh_d_done", "wd_ready", "wdT", "wt_ready",
                             "spread_done", "spread_ready"))
        h_done, h_ready, y_done, tmp_ready, ya_ready, fold_done, fin_ready, stored = (
            sem(n) for n in ("h_done", "h_ready", "y_done", "tmp_ready", "ya_ready", "fold_done", "fin_ready", "stored"))
        CONSTS = 8

        block = ctx.enter_context(nc.Block())

        @block.sync
        def _(sp):
            sp.dma_start(xt[:, 0:NT, :], x_tok[:, 0:NT, :]).then_inc(ld_xt0, 16)
            sp.dma_start(xt[:, NT:, :], x_tok[:, NT:, :]).then_inc(ld_xt1, 16)
            sp.dma_start(boff_bc[:, :], b_off.partition_broadcast(P)).then_inc(ld_boff, 16)
            for half in range(2):
                sp.dma_start(wdcn_raw[half * C:(half + 1) * C, :, :], w_dcn).then_inc(ld_wdcn, 16)
            sp.dma_start(xc[:, :, :], x_ch).then_inc(ld_xc, 16)
            for half in range(2):
                sp.dma_start(wg_raw[half * C:(half + 1) * C, :], wg).then_inc(ld_wg, 16)
            sp.dma_start(bg_bc[:, :], bg.partition_broadcast(P)).then_inc(ld_bias, 16)
            sp.dma_start(b1_col[:, :], b1).then_inc(ld_bias, 16)
            sp.dma_start(b2_col[:, :], b2).then_inc(ld_bias, 16)
            for half in range(2):
                sp.dma_start(w1_raw[half * C:(half + 1) * C, :, :], w1).then_inc(ld_w1, 16)
            sp.dma_start(w2_sb[:, :, :, :], w2).then_inc(ld_w2, 16)
            for b in range(NB):
                sp.wait_ge(fin_ready, b + 1)
                sp.dma_start(out[b], fin[:, b, :]).then_inc(stored, 16)
            sp.wait_ge(stored, 16 * NB)

        @block.gpsimd
        def _(pool):
            pool.memset(ident[:, :], 0.0).then_inc(pool_const, 1)
            pool.wait_ge(pool_const, 1)
            pool.affine_select(out=ident[:, :], in_=ident[:, :], compare_op=ALU.not_equal, fill=1.0, base=0,
                               pattern=[[-1, P]], channel_multiplier=1).then_inc(pool_const, 1)
            pool.memset(power[:, :], -0.5).then_inc(pool_const, 1)
            pool.iota(pidx[:, :], pattern=[[0, 1]], base=0, channel_multiplier=1).then_inc(pool_const, 1)
            pool.iota(grid[:, :], pattern=[[1, W]], base=0, channel_multiplier=0,
                      allow_small_or_imprecise_dtypes=True).then_inc(pool_const, 1)
            pool.iota(tapyx[:, 0:TAPS], pattern=[[1, KS], [0, KS]], base=-1, channel_multiplier=0,
                      allow_small_or_imprecise_dtypes=True).then_inc(pool_const, 1)
            pool.iota(tapyx[:, TAPS:], pattern=[[0, KS], [1, KS]], base=-1, channel_multiplier=0,
                      allow_small_or_imprecise_dtypes=True).then_inc(pool_const, 1)
            pool.memset(xpad[:, :, :, :].bitcast(F32), 0.0).then_inc(pool_const, 1)

            def rstd(var, src, dst, n, ready):
                pool.wait_ge(var, n)
                pool.wait_ge(pool_const, 3)
                pool.tensor_tensor(dst, src, power[:, 0:src.shape[1]], ALU.pow).then_inc(ready, 1)

            rstd(var1, ve1[:, 0:NT], rs1[:, 0:NT], 1, rstd1)
            rstd(var1, ve1[:, NT:], rs1[:, NT:], 2, rstd1)
            pool.iota(eight[:, :], pattern=[[1, E]], base=0, channel_multiplier=0,
                      allow_small_or_imprecise_dtypes=True).then_inc(sel_ready, 1)
            pool.memset(sel_f[:, :, :, :], 0.0).then_inc(pool_chain, 1)
            for i, row in enumerate((0, -E)):
                pool.wait_ge(pool_chain, i + 1)
                last = pool.affine_select(out=sel_f[:, :, :, :], in_=sel_f[:, :, :, :], compare_op=ALU.not_equal, fill=1.0,
                                          base=row, pattern=[[-2, PAIRS], [-1, 2], [0, O]], channel_multiplier=1)
                last.then_inc(pool_chain, 1)
            pool.wait_ge(pool_chain, 3)
            pool.tensor_copy(sel[:, :, :], sel_f[:, :, :, :].rearrange("r j e o -> r j (e o)")).then_inc(sel_ready, 1)

            def product(u):
                b, g = divmod(u, UNITS)
                if g == 0:
                    pool.wait_ge(haty_ready, b + 1)
                if u >= AT_RING:
                    pool.wait_ge(tap_T, GROUP * (u - AT_RING + 1))
                ks = slice(g * GROUP, (g + 1) * GROUP)
                pool.tensor_tensor(
                    at[:, u % AT_RING, 1, :, :].rearrange("p k (y x) -> p k y x", x=W),
                    haty[:, b % 2, 1, ks, :].unsqueeze(3).broadcast_to([P, GROUP, H, W]),
                    hats[:, b % 2, 1, TAPS + g * GROUP:TAPS + (g + 1) * GROUP, :].unsqueeze(2).broadcast_to([P, GROUP, H, W]),
                    ALU.mult).then_inc(at_pool, 1)

            product(0)
            pool.wait_ge(ld_w1, 32)
            for e in range(E):
                pool.tensor_copy(w1_hi[:, e, :], w1_raw[:, e, :]).then_inc(pool_chain, 1)
                if e in (0, 4):
                    product(1 + e // 4)
                pool.wait_ge(pool_chain, 4 + e)
                pool.tensor_tensor(w1_lo[:, e, :], w1_raw[:, e, :], w1_hi[:, e, :].bitcast(F32), ALU.subtract).then_inc(w1_ready, 1)

            for slot in range(LAST_SLOT + 1):
                if slot % GROUP == 0 and UNITS <= slot // GROUP + 1 < NB * UNITS:
                    product(slot // GROUP + 1)
                for task, b, *_ in tasks(slot):
                    if task == "stats":
                        rstd(var2, ve2[:, b % 2, :], rs2[:, b % 2, :], b + 1, rstd2)
                for b, i in ffn_steps(slot):
                    j = i // (2 * HC)
                    if i % (2 * HC) == 2 * HC - 1 and j > 0:
                        pool.wait_ge(tmp_ready, PAIRS * b + j + 1)
                        if j > 1:
                            pool.wait_ge(ya_ready, (PAIRS - 1) * b + j - 1)
                        elif b > 0:
                            pool.wait_ge(fold_done, b)
                        prev = tmp[:, 0, :] if j == 1 else ya[:, j - 2, :]
                        pool.tensor_tensor(ya[:, j - 1, :], prev, tmp[:, j, :], ALU.add).then_inc(ya_ready, 1)

        @block.scalar
        def _(act):
            for half in range(2):
                act.dma_start(woff_raw[half * C:(half + 1) * C, :, :], w_off).then_inc(ld_woff, 16)
            act.wait_ge(pool_const, 3)
            act.activation(tanh_d[:, 0:1], power[:, 0:1], ACT.Tanh).then_inc(act_chain, 1)
            chain = [1]

            def chained(ins):
                chain[0] += 1
                ins.then_inc(act_chain, 1)
                act.wait_ge(act_chain, chain[0])

            def pad_image(b, bank, col):
                act.wait_ge(xn1T, b + 1)
                act.wait_ge(pool_const, CONSTS)
                act.activation(xpad[:, b, 1:1 + H, 1:1 + W],
                               bank[:, col:col + HW].rearrange("p (y x) -> p y x", x=W), ACT.Copy).then_inc(xpad_ready, 1)
                act.activation(xflat[:, b, :], bank[:, col:col + HW], ACT.Copy).then_inc(xflat_ready, 1)

            def save_offsets(b):
                act.wait_ge(om_done, b + 1)
                act.activation(om_sb[:, b % 2, :], bank_p[0:2 * OM, 0:HW], ACT.Copy).then_inc(om_saved, 1)

            def hat_steps(b):
                act.wait_ge(pos_ready, b + 1)
                act.activation(tanh_m[:, b % 2, :, :], pos[:, b % 2, :, 2 * TAPS:], ACT.Tanh, scale=0.5).then_inc(tanh_done, 1)
                act.wait_ge(dist_ready, b + 1)
                chained(act.activation(adist[:, :, :, :], dist[:, :, :, :], ACT.Abs))
                act.activation(hats[:, b % 2, :, :, :], adist[:, :, :, :], ACT.Relu, bias=1.0, scale=-1.0).then_inc(hats_ready, 1)

            def value_hi(b, piece):
                st, k0, n = V_PIECES[piece]
                bank = V0_BANKS[piece] if b == 0 else bank_p
                act.wait_ge(v_done, len(V_PIECES) * b + piece + 1)
                act.activation(v_hl[:, b, st, k0:k0 + n, 0:O], bank[:, 0:n * O].rearrange("p (k o) -> p k o", o=O),
                               ACT.Copy).then_inc(v_hi, 1)

            pad_image(0, bank_p, 0)
            save_offsets(0)
            hat_steps(0)
            for piece in range(len(V_PIECES)):
                value_hi(0, piece)
            pad_image(1, bank_h[0], 0)
            pad_image(2, bank_h[0], HW)
            pad_image(3, bank_h[1], 0)
            for slot in range(LAST_SLOT + 1):
                if slot < SLOTS:
                    act.wait_ge(tap_T, slot + 1)
                    if slot >= A_RING:
                        act.wait_ge(tap_mm, slot - A_RING + 1)
                    act.activation(a_hi[:, slot % A_RING, :, :].rearrange("p s t -> p (s t)"), bank_t[slot % 2][:, :],
                                   ACT.Copy).then_inc(tap_hi, 1)
                for task, b, *more in tasks(slot):
                    if task == "conv":
                        save_offsets(b)
                    elif task == "offsets":
                        hat_steps(b)
                    elif task == "value":
                        value_hi(b, *more)
                    elif task == "residual":
                        act.wait_ge(tap_mm, TAPS * (b + 1))
                        if b >= 2:
                            act.wait_ge(t1_ready, b - 1)
                        act.activation(c1[:, b % 2, :], bank_o[O:2 * O, 0:HW], ACT.Copy).then_inc(lo_half, 1)
                    elif task == "stack":
                        act.wait_ge(xn2T, b + 1)
                        if b >= 2:
                            act.wait_ge(h_done, STEPS * (b - 1))
                        act.activation(x2s[:, b % 2, :], bank_c[:, 0:HW], ACT.Copy).then_inc(x2s_ready, 1)
                    elif task == "gate":
                        act.wait_ge(lg_done, b + 1)
                        act.activation(lg_sb[:, :], bank_c[0:2 * E, 0:HW], ACT.Copy).then_inc(lg_saved, 1)
                    elif task == "top":
                        act.wait_ge(diff_ready, b + 1)
                        act.activation(tanh_d[:, :], diff[:, :], ACT.Tanh, scale=0.5).then_inc(tanh_d_done, 1)
                    elif task == "weights":
                        act.wait_ge(wdT, b + 1)
                        act.activation(wt[:, :], bank_c[0:2 * E, 0:HW], ACT.Copy).then_inc(wt_ready, 1)
                    elif task == "spread":
                        half, = more
                        act.wait_ge(spread_done, 2 * b + half + 1)
                        if b >= 2:
                            act.wait_ge(tmp_ready, PAIRS * (b - 1))
                        act.activation(spread[:, b % 2, 2 * half:2 * half + 2, :].rearrange("p j t -> p (j t)"),
                                       bank_c[:, :], ACT.Copy).then_inc(spread_ready, 1)
                for b, i in ffn_steps(slot):
                    n = STEPS * b + i
                    act.wait_ge(h_done, n + 1)
                    if n == 0:
                        act.wait_ge(ld_bias, 48)
                    if n >= H_RING:
                        act.wait_ge(y_done, n - H_RING + 1)
                    act.activation(hid[:, n % H_RING, :], bank_h[n % 2][:, 0:HW], ACT.Gelu, bias=b1_col[:, i:i + 1]).then_inc(h_ready, 1)

        @block.vector
        def _(dve):
            chain = [0]

            def chained(ins):
                chain[0] += 1
                ins.then_inc(dve_chain, 1)
                dve.wait_ge(dve_chain, chain[0])

            def norm_stats(tiles, ready):
                for t in tiles:
                    last = dve.bn_stats(st1[:, t, :], xt[:, t, :])
                chained(last)
                for t in tiles:
                    last = dve.bn_aggr(mv1[:, t, :], st1[:, t, :])
                chained(last)
                a, z = tiles[0], tiles[-1] + 1
                dve.tensor_scalar(ve1[:, a:z], mv1[:, a:z, 1], LN_C_EPS, None, ALU.add).then_inc(ready, 1)

            def norm_apply(tiles, n):
                dve.wait_ge(rstd1, n)
                for t in tiles:
                    last = dve.tensor_scalar(xn1[:, t, :], xt[:, t, :], mv1[:, t, 0:1], rs1[:, t:t + 1], ALU.subtract, ALU.mult)
                chained(last)
                a, z = tiles[0], tiles[-1] + 1
                chained(dve.tensor_copy(xn1_hl[:, a:z, 0:C], xn1[:, a:z, :]))
                dve.tensor_tensor(xn1_hl[:, a:z, C:], xn1[:, a:z, :], xn1_hl[:, a:z, 0:C].bitcast(F32),
                                  ALU.subtract).then_inc(xn1_ready, 1)

            def make_base():
                dve.wait_ge(pool_const, 7)
                dve.tensor_scalar(prow_i[:, :], pidx[:, :], 4, None, ALU.arith_shift_right)
                chained(dve.tensor_scalar(pcol_i[:, :], pidx[:, :], W - 1, None, ALU.bitwise_and))
                dve.tensor_copy(prow[:, :], prow_i[:, :])
                chained(dve.tensor_copy(pcol[:, :], pcol_i[:, :]))
                dve.wait_ge(ld_boff, 16)
                chained(dve.tensor_scalar(tapyx[:, 0:TAPS], tapyx[:, 0:TAPS], prow[:, 0:1], None, ALU.add))
                chained(dve.tensor_scalar(tapyx[:, TAPS:], tapyx[:, TAPS:], pcol[:, 0:1], None, ALU.add))
                for j in range(NT):
                    dve.tensor_scalar(base[:, j, 0:TAPS], tapyx[:, 0:TAPS], float(j * RPT), None, ALU.add)
                    dve.tensor_copy(base[:, j, TAPS:2 * TAPS], tapyx[:, TAPS:])
                    last = dve.memset(base[:, j, 2 * TAPS:], 0.0)
                chained(last)
                dve.tensor_tensor(base[:, :, :], base[:, :, :], boff_bc[:, :].unsqueeze(1).broadcast_to([P, NT, OM]),
                                  ALU.add).then_inc(base_ready, 1)

            def positions(b):
                dve.wait_ge(omT, b + 1)
                chained(dve.tensor_tensor(pos_a[:, :, :], bank_p[:, 0:NT * 2 * OM].rearrange("p (j m) -> p j m", j=NT)[:, :, 0:OM],
                                          base[:, :, :], ALU.add))
                dve.tensor_tensor(pos[:, b % 2, :, :], bank_p[:, 0:NT * 2 * OM].rearrange("p (j m) -> p j m", j=NT)[:, :, OM:],
                                  pos_a[:, :, :], ALU.add).then_inc(pos_ready, 1)
                dve.wait_ge(pos_ready, b + 1)
                if b > 0:
                    dve.wait_ge(hats_ready, b)
                dve.tensor_tensor(dist[:, :, :, :],
                                  pos[:, b % 2, :, 0:2 * TAPS].unsqueeze(3).broadcast_to([P, NT, 2 * TAPS, W]),
                                  grid[:, :].unsqueeze(1).unsqueeze(1).broadcast_to([P, NT, 2 * TAPS, W]),
                                  ALU.subtract).then_inc(dist_ready, 1)

            def masked_hats(b):
                dve.wait_ge(tanh_done, b + 1)
                chained(dve.tensor_scalar(mask[:, b % 2, :, :], tanh_m[:, b % 2, :, :], 0.5, 0.5, ALU.mult, ALU.add))
                dve.wait_ge(hats_ready, b + 1)
                dve.tensor_tensor(haty[:, b % 2, :, :, :], hats[:, b % 2, :, 0:TAPS, :],
                                  mask[:, b % 2, :, :].unsqueeze(3).broadcast_to([P, NT, TAPS, H]), ALU.mult).then_inc(haty_ready, 1)

            def product(u):
                b, g = divmod(u, UNITS)
                if g == 0:
                    dve.wait_ge(haty_ready, b + 1)
                if u >= AT_RING:
                    dve.wait_ge(tap_T, GROUP * (u - AT_RING + 1))
                ks = slice(g * GROUP, (g + 1) * GROUP)
                dve.tensor_tensor(
                    at[:, u % AT_RING, 0, :, :].rearrange("p k (y x) -> p k y x", x=W),
                    haty[:, b % 2, 0, ks, :].unsqueeze(3).broadcast_to([P, GROUP, H, W]),
                    hats[:, b % 2, 0, TAPS + g * GROUP:TAPS + (g + 1) * GROUP, :].unsqueeze(2).broadcast_to([P, GROUP, H, W]),
                    ALU.mult).then_inc(at_dve, 1)

            def value_lo(b, piece):
                st, k0, n = V_PIECES[piece]
                bank = V0_BANKS[piece] if b == 0 else bank_p
                dve.wait_ge(v_hi, len(V_PIECES) * b + piece + 1)
                dve.tensor_tensor(v_hl[:, b, st, k0:k0 + n, O:], bank[:, 0:n * O].rearrange("p (k o) -> p k o", o=O),
                                  v_hl[:, b, st, k0:k0 + n, 0:O].bitcast(F32), ALU.subtract).then_inc(v_lo, 1)

            def split(hi, lo, raw, ready):
                chained(dve.tensor_copy(hi, raw))
                dve.tensor_tensor(lo, raw, hi.bitcast(F32), ALU.subtract).then_inc(ready, 1)

            first, rest = list(range(NT)), list(range(NT, NB * NT))
            dve.wait_ge(ld_xt0, 16)
            norm_stats(first, var1)
            dve.wait_ge(ld_woff, 32)
            split(woff[:, :, 0:OM], woff[:, :, OM:], woff_raw[:, :, :], woff_ready)
            norm_apply(first, 1)
            make_base()
            dve.wait_ge(ld_wdcn, 32)
            split(wdcn_hi[:, :, :], wdcn_lo[:, :, :], wdcn_raw[:, :, :], wdcn_ready)
            dve.wait_ge(base_ready, 1)
            positions(0)
            dve.wait_ge(ld_xt1, 16)
            norm_stats(rest, var1)
            masked_hats(0)
            product(0)
            for piece in range(len(V_PIECES)):
                value_lo(0, piece)
            norm_apply(rest, 2)
            product(1)
            product(2)
            dve.wait_ge(ld_wg, 32)
            split(wg_hl[:, 0:E], wg_hl[:, E:], wg_raw[:, :], wg_ready)
            dve.tensor_copy(fold[0:O, :], ident[0:O, 0:O])
            dve.tensor_copy(fold[O:, :], ident[O:, O:]).then_inc(fold_ready, 1)

            for slot in range(LAST_SLOT + 1):
                if slot < SLOTS:
                    dve.wait_ge(tap_hi, slot + 1)
                    dve.tensor_tensor(a_lo[:, slot % A_RING, :, :].rearrange("p s t -> p (s t)"), bank_t[slot % 2][:, :],
                                      a_hi[:, slot % A_RING, :, :].bitcast(F32).rearrange("p s t -> p (s t)"),
                                      ALU.subtract).then_inc(tap_lo, 1)
                if slot % GROUP == 0 and UNITS <= slot // GROUP + 1 < NB * UNITS:
                    product(slot // GROUP + 1)
                for task, b, *more in tasks(slot):
                    if task == "offsets":
                        positions(b)
                    elif task == "mask":
                        masked_hats(b)
                    elif task == "value":
                        value_lo(b, *more)
                    elif task == "residual":
                        if b == 0:
                            dve.wait_ge(ld_xc, 16)
                        dve.wait_ge(lo_half, b + 1)
                        chained(dve.tensor_tensor(c2[:, b % 2, :], c1[:, b % 2, :], xc[:, b, :], ALU.add))
                        dve.tensor_tensor(t1[:, b, :], bank_o[0:O, 0:HW], c2[:, b % 2, :], ALU.add).then_inc(t1_ready, 1)
                    elif task == "stats":
                        dve.wait_ge(t1T, b + 1)
                        for j in range(NT):
                            last = dve.bn_stats(st2[:, j, :], bank_c[:, j * O:(j + 1) * O])
                        chained(last)
                        for j in range(NT):
                            last = dve.bn_aggr(mv2[:, b % 2, j, :], st2[:, j, :])
                        chained(last)
                        dve.tensor_scalar(ve2[:, b % 2, :], mv2[:, b % 2, :, 1], LN_T_EPS, None, ALU.add).then_inc(var2, 1)
                    elif task == "norm":
                        dve.wait_ge(rstd2, b + 1)
                        for j in range(NT):
                            last = dve.tensor_scalar(xn2[:, j, :], bank_c[:, j * O:(j + 1) * O], mv2[:, b % 2, j, 0:1],
                                                     rs2[:, b % 2, j:j + 1], ALU.subtract, ALU.mult)
                        chained(last)
                        if b > 0:
                            dve.wait_ge(xn2T, b)
                        split(xn2_hl[:, :, 0:C], xn2_hl[:, :, C:], xn2[:, :, :], xn2_ready)
                    elif task == "top":
                        dve.wait_ge(lgT, b + 1)
                        if b == 0:
                            dve.wait_ge(ld_bias, 48)
                        lg = bank_c[:, 0:NT * 2 * E].rearrange("p (j m) -> p j m", j=NT)
                        chained(dve.tensor_tensor(lg_a[:, :, :], lg[:, :, 0:E],
                                                  bg_bc[:, :].unsqueeze(1).broadcast_to([P, NT, E]), ALU.add))
                        chained(dve.tensor_tensor(logit[:, :, :], lg[:, :, E:], lg_a[:, :, :], ALU.add))
                        for j in range(NT):
                            last = dve.max(top[:, j, :], logit[:, j, :])
                        chained(last)
                        dve.tensor_tensor(diff[:, :], top[:, :, 0], top[:, :, 1], ALU.subtract).then_inc(diff_ready, 1)
                        for j in range(NT):
                            last = dve.max_index(topi[:, j, :], top[:, j, :], logit[:, j, :])
                        chained(last)
                        chained(dve.tensor_copy(topf[:, :, :], topi[:, :, 0:2]))
                        if b == 0:
                            dve.wait_ge(sel_ready, 1)
                        dve.tensor_tensor(onehot[:, :, :, :], eight[:, :].unsqueeze(1).unsqueeze(1).broadcast_to([P, NT, 2, E]),
                                          topf[:, :, :].unsqueeze(3).broadcast_to([P, NT, 2, E]), ALU.is_equal)
                        dve.wait_ge(tanh_d_done, b + 1)
                        dve.tensor_scalar(pw[:, :, 0], tanh_d[:, :], 0.5, 0.5, ALU.mult, ALU.add)
                        chained(dve.tensor_scalar(pw[:, :, 1], tanh_d[:, :], -0.5, 0.5, ALU.mult, ALU.add))
                        chained(dve.tensor_tensor(gated[:, :, :, :], onehot[:, :, :, :],
                                                  pw[:, :, :].unsqueeze(3).broadcast_to([P, NT, 2, E]), ALU.mult))
                        chained(dve.tensor_tensor(wd[:, :, :], gated[:, :, 0, :], gated[:, :, 1, :], ALU.add))
                        split(wd_hl[:, :, 0:E], wd_hl[:, :, E:], wd[:, :, :], wd_ready)
                for b, i in ffn_steps(slot):
                    if i % (2 * HC) == 2 * HC - 1:
                        j = i // (2 * HC)
                        dve.wait_ge(y_done, STEPS * b + i + 1)
                        dve.wait_ge(spread_ready, 2 * b + j // 2 + 1)
                        if b > 0:
                            dve.wait_ge(ya_ready, (PAIRS - 1) * (b - 1) + max(j, 1))
                        dve.scalar_tensor_tensor(tmp[:, j, :], bank_y[:, 0:HW], b2_col[:, j:j + 1], spread[:, b % 2, j, :],
                                                 ALU.add, ALU.mult).then_inc(tmp_ready, 1)
                    if i == STEPS - 1:
                        dve.wait_ge(fold_done, b + 1)
                        dve.tensor_tensor(fin[:, b, :], bank_c[0:O, 0:HW], t1[:, b, :], ALU.add).then_inc(fin_ready, 1)

        @block.tensor
        def _(pe):
            released = {}

            def take(name, sem_, value):
                if name in released:
                    pe.wait_ge(*released[name])
                released[name] = (sem_, value)

            def transpose_xn(b, bank, col):
                pe.wait_ge(xn1_ready, 1 if b == 0 else 2)
                for j in range(NT):
                    last = pe.transpose(bank[:, col + j * P:col + (j + 1) * P], xn1_hl[:, NT * b + j, :].bitcast(F32), ident[:, :])
                last.then_inc(xn1T, 1)

            def conv(b):
                take("p", om_saved, b + 1)
                pe.wait_ge(xpad_ready, b + 1)
                for k in range(TAPS):
                    ky, kx = divmod(k, KS)
                    last = pe.matmul(bank_p[0:2 * OM, 0:HW], woff[:, k, :], xpad[:, b, ky:ky + H, kx:kx + W],
                                     start=(k == 0), stop=(k == TAPS - 1))
                last.then_inc(om_done, 1)

            def transpose_om(b):
                take("p", pos_ready, b + 1)
                for j in range(NT):
                    last = pe.transpose(bank_p[:, j * 2 * OM:(j + 1) * 2 * OM], om_sb[:, b % 2, j * P:(j + 1) * P],
                                        ident[0:2 * OM, 0:2 * OM])
                last.then_inc(omT, 1)

            def value(b, piece):
                st, k0, n = V_PIECES[piece]
                count = len(V_PIECES) * b + piece + 1
                if b == 0:
                    bank = V0_BANKS[piece]
                    released[("c", "y", "o", "h1")[piece]] = (v_lo, count)
                else:
                    bank = bank_p
                    take("p", v_lo, count)
                pe.wait_ge(wdcn_ready, 1)
                pe.wait_ge(xflat_ready, b + 1)
                src = xflat[:, b, st * P:(st + 1) * P]
                pe.matmul(bank[:, 0:n * O], src, wdcn_hi[:, k0:k0 + n, :], start=True, stop=False)
                pe.matmul(bank[:, 0:n * O], src, wdcn_lo[:, k0:k0 + n, :], start=False, stop=True).then_inc(v_done, 1)

            pe.wait_ge(pool_const, 2)
            released["p"] = (xflat_ready, 1)
            transpose_xn(0, bank_p, 0)
            pe.wait_ge(woff_ready, 1)
            conv(0)
            transpose_om(0)
            for piece in range(len(V_PIECES)):
                value(0, piece)
            transpose_xn(1, bank_h[0], 0)
            pe.wait_ge(xflat_ready, 2)
            transpose_xn(2, bank_h[0], HW)
            pe.wait_ge(v_lo, len(V_PIECES))
            transpose_xn(3, bank_h[1], 0)

            def sample(slot):
                b, k = divmod(slot, TAPS)
                pe.wait_ge(tap_lo, slot + 1)
                if k == 0:
                    pe.wait_ge(v_lo, len(V_PIECES) * (b + 1))
                    if b > 0:
                        pe.wait_ge(t1_ready, b)
                for st in range(ST):
                    for part in (a_hi, a_lo):
                        last = pe.matmul(bank_o[:, 0:HW], v_hl[:, b, st, k, :], part[:, slot % A_RING, st, :],
                                         start=(k == 0 and st == 0 and part is a_hi),
                                         stop=(k == TAPS - 1 and st == ST - 1 and part is a_lo))
                last.then_inc(tap_mm, 1)

            def hidden(b, i):
                n = STEPS * b + i
                e, c = divmod(i, HC)
                if n == 0:
                    pe.wait_ge(w1_ready, E)
                    pe.wait_ge(xflat_ready, NB)
                if i == 0:
                    pe.wait_ge(x2s_ready, b + 1)
                if n >= 2:
                    pe.wait_ge(h_ready, n - 1)
                pe.matmul(bank_h[n % 2][:, 0:HW], w1_hi[:, e, c * P:(c + 1) * P], x2s[:, b % 2, :], start=True, stop=False)
                pe.matmul(bank_h[n % 2][:, 0:HW], w1_lo[:, e, c * P:(c + 1) * P], x2s[:, b % 2, :], start=False, stop=True).then_inc(h_done, 1)

            def expert_out(n):
                b, i = divmod(n, STEPS)
                e, c = divmod(i, HC)
                if n == 0:
                    pe.wait_ge(ld_w2, 16)
                if i % (2 * HC) == 0:
                    take("y", tmp_ready, PAIRS * b + i // (2 * HC) + 1)
                pe.wait_ge(h_ready, n + 1)
                half = O * (e % 2)
                pe.matmul(bank_y[half:half + O, 0:HW], w2_sb[:, e, c, :], hid[:, n % H_RING, :],
                          start=(c == 0), stop=(c == HC - 1)).then_inc(y_done, 1)
                if i == STEPS - 1:
                    take("c", fin_ready, b + 1)
                    pe.wait_ge(ya_ready, (PAIRS - 1) * (b + 1))
                    pe.wait_ge(fold_ready, 1)
                    pe.matmul(bank_c[0:O, 0:HW], fold[:, :], ya[:, PAIRS - 2, :], start=True, stop=True).then_inc(fold_done, 1)

            pending = []
            for slot in range(LAST_SLOT + 1):
                if slot < SLOTS:
                    if slot % GROUP == 0:
                        pe.wait_ge(at_dve, slot // GROUP + 1)
                        pe.wait_ge(at_pool, slot // GROUP + 1)
                    if slot >= 2:
                        pe.wait_ge(tap_lo, slot - 1)
                    for st in range(ST):
                        for j in range(NT):
                            last = pe.transpose(bank_t[slot % 2][:, st * HW + j * P:st * HW + (j + 1) * P],
                                                at[:, slot // GROUP % AT_RING, j, slot % GROUP, st * P:(st + 1) * P], ident[:, :])
                    last.then_inc(tap_T, 1)
                if 1 <= slot <= SLOTS:
                    sample(slot - 1)
                for task, b, *more in tasks(slot):
                    if task == "conv":
                        conv(b)
                    elif task == "offsets":
                        pe.wait_ge(om_saved, b + 1)
                        transpose_om(b)
                    elif task == "value":
                        value(b, *more)
                    elif task == "stats":
                        take("c", xn2_ready, b + 1)
                        pe.wait_ge(t1_ready, b + 1)
                        for j in range(NT):
                            last = pe.transpose(bank_c[:, j * O:(j + 1) * O], t1[:, b, j * P:(j + 1) * P], ident[0:O, 0:O])
                        last.then_inc(t1T, 1)
                    elif task == "stack":
                        take("c", x2s_ready, b + 1)
                        pe.wait_ge(xn2_ready, b + 1)
                        for j in range(NT):
                            last = pe.transpose(bank_c[:, j * P:(j + 1) * P], xn2_hl[:, j, :].bitcast(F32), ident[:, :])
                        last.then_inc(xn2T, 1)
                    elif task == "gate":
                        take("c", lg_saved, b + 1)
                        pe.wait_ge(wg_ready, 1)
                        pe.wait_ge(x2s_ready, b + 1)
                        pe.matmul(bank_c[0:2 * E, 0:HW], wg_hl[:, :], x2s[:, b % 2, :], start=True, stop=True).then_inc(lg_done, 1)
                    elif task == "top":
                        pe.wait_ge(lg_saved, b + 1)
                        take("c", wd_ready, b + 1)
                        for j in range(NT):
                            last = pe.transpose(bank_c[:, j * 2 * E:(j + 1) * 2 * E], lg_sb[:, j * P:(j + 1) * P], ident[0:2 * E, 0:2 * E])
                        last.then_inc(lgT, 1)
                    elif task == "weights":
                        take("c", wt_ready, b + 1)
                        pe.wait_ge(wd_ready, b + 1)
                        for j in range(NT):
                            last = pe.transpose(bank_c[0:2 * E, j * P:(j + 1) * P], wd_hl[:, j, :].bitcast(F32), ident[:, :])
                        last.then_inc(wdT, 1)
                    elif task == "spread":
                        half, = more
                        take("c", spread_ready, 2 * b + half + 1)
                        pe.wait_ge(wt_ready, b + 1)
                        pe.wait_ge(sel_ready, 2)
                        for j in range(2):
                            last = pe.matmul(bank_c[:, j * HW:(j + 1) * HW], sel[:, 2 * half + j, :], wt[:, :], start=True, stop=True)
                        last.then_inc(spread_done, 1)
                for b, i in ffn_steps(slot):
                    hidden(b, i)
                    pending.append(STEPS * b + i)
                    if len(pending) > 1:
                        expert_out(pending.pop(0))
            while pending:
                expert_out(pending.pop(0))


def kernel(**inputs):
    import numpy as np
    import concourse.bacc as bacc
    from concourse.bass_utils import run_bass_kernel_spmd

    x = np.asarray(inputs["x"])
    w_off = np.asarray(inputs["L0_conv_w_off"])
    b_off = np.asarray(inputs["L0_conv_b_off"])
    order = np.concatenate([np.arange(TAPS) * 2, np.arange(TAPS) * 2 + 1, np.arange(2 * TAPS, 3 * TAPS)])
    arrays = {
        "x_tok": x.reshape(NB, C, NT, P).transpose(3, 0, 2, 1).reshape(P, NB * NT, C),
        "x_ch": x.reshape(NB, C, HW).transpose(1, 0, 2),
        "w_off": w_off[order].reshape(OM, C, TAPS).transpose(1, 2, 0),
        "b_off": b_off[order],
        "w_dcn": np.asarray(inputs["L0_conv_w_dcn"]).reshape(O, C, TAPS).transpose(1, 2, 0),
        "wg": np.asarray(inputs["L0_ffn_Wg"]),
        "bg": np.asarray(inputs["L0_ffn_bg"]),
        "w1": np.asarray(inputs["L0_ffn_W1"]).transpose(1, 0, 2),
        "b1": np.asarray(inputs["L0_ffn_b1"]).reshape(STEPS, P).T,
        "w2": np.asarray(inputs["L0_ffn_W2"]).reshape(E, HC, P, O).transpose(2, 0, 1, 3),
        "b2": np.asarray(inputs["L0_ffn_b2"]).reshape(PAIRS, 2 * O).T,
    }
    arrays = {f"in_{n}": np.ascontiguousarray(a) for n, a in arrays.items()}
    nc = bacc.Bacc("TRN2", target_bir_lowering=False, num_devices=1)
    args = [nc.dram_tensor(n, a.shape, mybir.dt.from_np(a.dtype), kind="ExternalInput").ap() for n, a in arrays.items()]
    out = nc.dram_tensor("out_0", (NB, C, HW), F32, kind="ExternalOutput").ap()
    metaformer_kernel(nc, *args, out)
    r = run_bass_kernel_spmd(nc, [arrays], core_ids=[0])
    return r.results[0]["out_0"].reshape(NB, C, H, W)
```

```python
from contextlib import ExitStack

import concourse.bass as bass
from concourse import mybir

F32 = mybir.dt.float32
F32R = mybir.dt.float32r
I32 = mybir.dt.int32
U32 = mybir.dt.uint32
ACT = mybir.ActivationFunctionType
ALU = mybir.AluOpType

P = 128
NB, C, H, W = 4, 64, 16, 16
HW = H * W
NT = HW // P
KS = 3
TAPS = KS * KS
OM = 3 * TAPS
O = 64
E, HID = 8, 256
HC = HID // P
PAIRS = E // 2
ST = HW // P
RPT = P // W
HP, WP = H + 2, W + 2
GROUP = 3
UNITS = TAPS // GROUP
SLOTS = NB * TAPS
TAP_BEATS = 4
BEATS = TAP_BEATS * TAPS
STEPS = E * HC
W1_CHUNKS = 4
V_PIECES = [(st, lo, n) for st in range(ST) for lo, n in ((0, 5), (5, 4))]
LN_C_EPS, LN_T_EPS = 1e-6, 1e-5
AT_RING, A_RING, H_RING = 4, 6, 3
T_WIDE = 12
LAG = 2
WARM = 12


PE_AT = dict(tap=0, sample=8, conv=-32, om=-28, value=-17, t1=43, stack=54, gate=58, logits=60, weights=71, spread0=74,
               spread1=78, xn=-36)
ACT_AT = dict(hi=0, hats=-20, conv=-31, value=-17, half=40, stack=54, gate=(62, 56, 56, 56), tanh=64, weights=70, spread0=74,
               spread1=78, pad=-34)
DVE_AT = dict(lo=4, positions=-27, value=-15, product=(0, 0, 0, 0, 0, 6, 6, 6, 6, 6, 6, 6), residual=41, stats=44, norm=48,
               top=64, gates=66, xn=-36)
POOL_AT = dict(dist=-22, haty=-20, product=3, rstd=42)
SETUP_AT = dict(w1_hi0=10, w1_hi1=22, w1_hi2=26, w1_hi3=32, w1_lo0=36, w1_lo1=42, w1_lo2=53, w1_lo3=58, sel=30, v0_0=3, v0_1=3,
               v0_2=7, v0_3=7)
VALUE_STEP = 5
FFN_AT = [[62, 64, 66, 68, 69, 74, 76, 78, 78, 82, 84, 88, 92, 94, 96, 96],
          [62, 64, 66, 68, 69, 74, 76, 78, 80, 82, 87, 91, 92, 94, 96, 96],
          [62, 64, 66, 68, 71, 76, 78, 80, 80, 83, 84, 88, 92, 94, 96, 96],
          [61, 64, 65, 67, 69, 72, 72, 74, 76, 79, 80, 80, 80, 81, 81, 81]]
POOL_TILES = [(1,), (0, 1), (1,), (0, 1), (0, 1), (1,), (0, 1), (0, 1), (1,), (1,), (0, 1), (0, 1)]
LAST_BEAT = BEATS * (NB - 1) + FFN_AT[-1][-1]


def due(beat, offset, first=0):
    offsets = (offset,) * NB if isinstance(offset, int) else offset
    return [b for b in range(first, NB) if BEATS * b + offsets[b] == beat]


def setup_due(beat, name):
    return [i for i in range(W1_CHUNKS) if SETUP_AT[f"{name}{i}"] == beat]


def taps_due(beat, offset=0):
    slot, rest = divmod(beat - offset, TAP_BEATS)
    return [slot] if rest == 0 and 0 <= slot < SLOTS else []


def pieces_due(beat, offset):
    offsets = (offset,) * NB if isinstance(offset, int) else offset
    return [(b, piece) for b in range(1, NB) for piece in range(len(V_PIECES))
            if BEATS * b + offsets[b] + VALUE_STEP * piece == beat]


def units_due(beat, offset):
    offsets = (offset,) * NB * UNITS if isinstance(offset, int) else offset
    return [u for u in range(1, NB * UNITS) if TAP_BEATS * GROUP * (u - 1) + offsets[u] == beat]


def on_pool(u, j):
    return j in POOL_TILES[u]


def made(slot, pool):
    if slot < GROUP:
        return slot + 1
    return GROUP + sum(on_pool(u, j) is pool for u in range(1, slot // GROUP + 1) for j in range(NT))


def ffn_steps(beat):
    return [(b, i) for b in range(NB) for i in range(STEPS) if BEATS * b + FFN_AT[b][i] == beat]


def second_products(beat):
    def through(s):
        first = sum(BEATS * b + FFN_AT[b][i] <= s for b in range(NB) for i in range(STEPS))
        return first if s == LAST_BEAT else max(0, first - LAG)
    return [divmod(n, STEPS) for n in range(through(beat - 1), through(beat))]


def metaformer_kernel(nc, x_tok, x_ch, w_off, b_off, w_dcn, wg, bg, w1, b1, w2, b2, out):
    ctx = ExitStack()
    with ctx:
        def sb(name, shape, dt=F32):
            return ctx.enter_context(nc.sbuf_tensor(name, shape, dt))

        def ps(name):
            return ctx.enter_context(nc.psum_tensor(name, [P, 512], F32))

        def sem(name):
            return ctx.enter_context(nc.semaphore(name))

        xt = sb("xt", [P, NB * NT, C])
        xc = sb("xc", [C, NB, HW])
        woff_raw = sb("woff_raw", [P, TAPS, OM])
        wdcn_raw = sb("wdcn_raw", [P, TAPS, O])
        w1_raw = sb("w1_raw", [P, E, HID])
        wg_raw = sb("wg_raw", [P, E])
        boff_bc = sb("boff_bc", [P, OM])
        bg_bc = sb("bg_bc", [P, E])
        b1_col = sb("b1_col", [P, STEPS])
        b2_col = sb("b2_col", [P, PAIRS])
        w2_sb = sb("w2_sb", [P, E, HC, O])
        woff = sb("woff", [P, TAPS, 2 * OM], F32R)
        wdcn_hi = sb("wdcn_hi", [P, TAPS, O], F32R)
        wdcn_lo = sb("wdcn_lo", [P, TAPS, O], F32R)
        w1_hi = sb("w1_hi", [P, E, HID], F32R)
        w1_lo = sb("w1_lo", [P, E, HID], F32R)
        wg_hl = sb("wg_hl", [P, 2 * E], F32R)
        ident = sb("ident", [P, P])
        fold = sb("fold", [P, O])
        sel_f = sb("sel_f", [2 * E, PAIRS, 2, O])
        sel = sb("sel", [2 * E, PAIRS, 2 * O], F32R)
        grid = sb("grid", [P, W])
        eight = sb("eight", [P, E])
        power = sb("power", [P, NB * NT])
        pidx = sb("pidx", [P, 1], I32)
        prow_i = sb("prow_i", [P, 1], I32)
        pcol_i = sb("pcol_i", [P, 1], I32)
        prow = sb("prow", [P, 1])
        pcol = sb("pcol", [P, 1])
        tapyx = sb("tapyx", [P, 2 * TAPS])
        base = sb("base", [P, NT, OM])
        st1 = sb("st1", [P, NB * NT, 6])
        mv1 = sb("mv1", [P, NB * NT, 2])
        ve1 = sb("ve1", [P, NB * NT])
        rs1 = sb("rs1", [P, NB * NT])
        xn1 = sb("xn1", [P, NB * NT, C])
        xn1_hl = sb("xn1_hl", [P, NB * NT, 2 * C], F32R)
        xpad = sb("xpad", [P, NB, HP, WP], F32R)
        xflat = sb("xflat", [P, NB, HW], F32R)
        om_sb = sb("om_sb", [2 * OM, 2, HW])
        pos_a = sb("pos_a", [P, NT, OM])
        pos = sb("pos", [P, 2, NT, OM])
        tanh_m = sb("tanh_m", [P, 2, NT, TAPS])
        mask = sb("mask", [P, 2, NT, TAPS])
        dist = sb("dist", [P, NT, 2 * TAPS, W])
        adist = sb("adist", [P, NT, 2 * TAPS, W])
        hats = sb("hats", [P, 2, NT, 2 * TAPS, W])
        haty = sb("haty", [P, 2, NT, TAPS, W])
        at = sb("at", [P, AT_RING, NT, GROUP, HW])
        a_hi = sb("a_hi", [P, A_RING, ST, HW], F32R)
        a_lo = sb("a_lo", [P, A_RING, ST, HW], F32R)
        v_hl = sb("v_hl", [P, NB, ST, TAPS, 2 * O], F32R)
        c1 = sb("c1", [O, 2, HW])
        c2 = sb("c2", [O, 2, HW])
        t1 = sb("t1", [O, NB, HW])
        st2 = sb("st2", [P, NT, 6])
        mv2 = sb("mv2", [P, 2, NT, 2])
        ve2 = sb("ve2", [P, 2, NT])
        rs2 = sb("rs2", [P, 2, NT])
        xn2 = sb("xn2", [P, NT, C])
        xn2_hl = sb("xn2_hl", [P, NT, 2 * C], F32R)
        x2s = sb("x2s", [P, 2, HW], F32R)
        lg_sb = sb("lg_sb", [2 * E, HW])
        lg_a = sb("lg_a", [P, NT, E])
        logit = sb("logit", [P, NT, E])
        top = sb("top", [P, NT, 8])
        topi = sb("topi", [P, NT, 8], U32)
        topf = sb("topf", [P, NT, 2])
        diff = sb("diff", [P, NT])
        tanh_d = sb("tanh_d", [P, NT])
        pw = sb("pw", [P, NT, 2])
        onehot = sb("onehot", [P, NT, 2, E])
        gated = sb("gated", [P, NT, 2, E])
        wd = sb("wd", [P, NT, E])
        wd_hl = sb("wd_hl", [P, NT, 2 * E], F32R)
        wt = sb("wt", [2 * E, HW], F32R)
        spread = sb("spread", [P, 2, PAIRS, HW])
        hid = sb("hid", [P, H_RING, HW])
        tmp = sb("tmp", [P, PAIRS, HW])
        ya = sb("ya", [P, 3, HW])
        fin = sb("fin", [O, NB, HW])

        bank_t = [ps("bank_t0"), ps("bank_t1")]
        bank_o = ps("bank_o")
        bank_p = ps("bank_p")
        bank_c = ps("bank_c")
        bank_h = [ps("bank_h0"), ps("bank_h1")]
        bank_y = ps("bank_y")
        Y_BANKS = [[bank_y] * PAIRS] * (NB - 1) + [[bank_y, bank_p, *bank_t]]

        def t_bank(slot):
            return (bank_t + bank_h)[slot % 4] if slot < T_WIDE else bank_t[slot % 2]

        V0_BANKS = [bank_c, bank_y, bank_o, bank_h[1]]

        ld_xt0, ld_xt1, ld_xc, ld_woff, ld_wdcn = (sem(n) for n in ("ld_xt0", "ld_xt1", "ld_xc", "ld_woff", "ld_wdcn"))
        ld_w1, ld_w2, ld_wg, ld_boff, ld_bias = (sem(n) for n in ("ld_w1", "ld_w2", "ld_wg", "ld_boff", "ld_bias"))
        pool_const = sem("pool_const")
        base_ready, woff_ready, wdcn_ready, wg_ready, w1_ready, fold_ready, sel_ready = (
            sem(n) for n in ("base_ready", "woff_ready", "wdcn_ready", "wg_ready", "w1_ready", "fold_ready", "sel_ready"))
        hats0_ready = [sem("hats0_ready0"), sem("hats0_ready1")]
        wdcn_hi_ready, w1_hi_ready, mask_ready = sem("wdcn_hi_ready"), sem("w1_hi_ready"), sem("mask_ready")
        dve_chain, act_chain, pool_chain = sem("dve_chain"), sem("act_chain"), sem("pool_chain")
        var1, rstd1, xn1_ready, xn1T, xpad_ready, xflat_ready = (
            sem(n) for n in ("var1", "rstd1", "xn1_ready", "xn1T", "xpad_ready", "xflat_ready"))
        om_done, om_saved, omT, pos_ready, tanh_done, dist_ready, hats_ready, haty_ready = (
            sem(n) for n in ("om_done", "om_saved", "omT", "pos_ready", "tanh_done", "dist_ready", "hats_ready", "haty_ready"))
        v_done, v_hi, v_lo = sem("v_done"), sem("v_hi"), sem("v_lo")
        at_dve, at_pool = sem("at_dve"), sem("at_pool")
        tap_T, tap_hi, tap_lo, tap_mm = sem("tap_T"), sem("tap_hi"), sem("tap_lo"), sem("tap_mm")
        lo_half, t1_ready, t1T, var2, rstd2, xn2_ready, xn2T, x2s_ready = (
            sem(n) for n in ("lo_half", "t1_ready", "t1T", "var2", "rstd2", "xn2_ready", "xn2T", "x2s_ready"))
        lg_done, lg_saved, lgT, logit_ready, diff_ready, tanh_d_done, wd_ready, wdT, wt_ready, spread_done, spread_ready = (
            sem(n) for n in ("lg_done", "lg_saved", "lgT", "logit_ready", "diff_ready", "tanh_d_done", "wd_ready", "wdT", "wt_ready",
                             "spread_done", "spread_ready"))
        h_done, h_ready, y_done, tmp_ready, ya_ready, fold_done, fin_ready, stored = (
            sem(n) for n in ("h_done", "h_ready", "y_done", "tmp_ready", "ya_ready", "fold_done", "fin_ready", "stored"))
        CONSTS = 8

        block = ctx.enter_context(nc.Block())

        @block.sync
        def _(sp):
            sp.dma_start(xt[:, 0:NT, :], x_tok[:, 0:NT, :]).then_inc(ld_xt0, 16)
            sp.dma_start(xt[:, NT:, :], x_tok[:, NT:, :]).then_inc(ld_xt1, 16)
            sp.dma_start(boff_bc[:, :], b_off.partition_broadcast(P)).then_inc(ld_boff, 16)
            for half in range(2):
                sp.dma_start(wdcn_raw[half * C:(half + 1) * C, :, :], w_dcn).then_inc(ld_wdcn, 16)
            sp.dma_start(xc[:, :, :], x_ch).then_inc(ld_xc, 16)
            for half in range(2):
                sp.dma_start(wg_raw[half * C:(half + 1) * C, :], wg).then_inc(ld_wg, 16)
            sp.dma_start(bg_bc[:, :], bg.partition_broadcast(P)).then_inc(ld_bias, 16)
            sp.dma_start(b1_col[:, :], b1).then_inc(ld_bias, 16)
            sp.dma_start(b2_col[:, :], b2).then_inc(ld_bias, 16)
            for half in range(2):
                sp.dma_start(w1_raw[half * C:(half + 1) * C, :, :], w1).then_inc(ld_w1, 16)
            sp.dma_start(w2_sb[:, :, :, :], w2).then_inc(ld_w2, 16)
            for b in range(NB):
                sp.wait_ge(fin_ready, b + 1)
                sp.dma_start(out[b], fin[:, b, :]).then_inc(stored, 16)
            sp.wait_ge(stored, 16 * NB)

        @block.gpsimd
        def _(pool):
            pool.memset(ident[:, :], 0.0).then_inc(pool_const, 1)
            pool.wait_ge(pool_const, 1)
            pool.affine_select(out=ident[:, :], in_=ident[:, :], compare_op=ALU.not_equal, fill=1.0, base=0,
                               pattern=[[-1, P]], channel_multiplier=1).then_inc(pool_const, 1)
            pool.memset(power[:, :], -0.5).then_inc(pool_const, 1)
            pool.iota(pidx[:, :], pattern=[[0, 1]], base=0, channel_multiplier=1).then_inc(pool_const, 1)
            pool.iota(grid[:, :], pattern=[[1, W]], base=0, channel_multiplier=0,
                      allow_small_or_imprecise_dtypes=True).then_inc(pool_const, 1)
            pool.iota(tapyx[:, 0:TAPS], pattern=[[1, KS], [0, KS]], base=-1, channel_multiplier=0,
                      allow_small_or_imprecise_dtypes=True).then_inc(pool_const, 1)
            pool.iota(tapyx[:, TAPS:], pattern=[[0, KS], [1, KS]], base=-1, channel_multiplier=0,
                      allow_small_or_imprecise_dtypes=True).then_inc(pool_const, 1)
            pool.memset(xpad[:, :, :, :].bitcast(F32), 0.0).then_inc(pool_const, 1)

            def rstd(var, src, dst, n, ready):
                pool.wait_ge(var, n)
                pool.wait_ge(pool_const, 3)
                pool.tensor_tensor(dst, src, power[:, 0:src.shape[1]], ALU.pow).then_inc(ready, 1)

            rstd(var1, ve1[:, 0:NT], rs1[:, 0:NT], 1, rstd1)

            pool.memset(sel_f[:, :, :, :], 0.0).then_inc(pool_chain, 1)
            for i, row in enumerate((0, -E)):
                pool.wait_ge(pool_chain, i + 1)
                pool.affine_select(out=sel_f[:, :, :, :], in_=sel_f[:, :, :, :], compare_op=ALU.not_equal, fill=1.0,
                                   base=row, pattern=[[-2, PAIRS], [-1, 2], [0, O]], channel_multiplier=1).then_inc(pool_chain, 1)
            pool.wait_ge(wdcn_hi_ready, 1)
            pool.tensor_tensor(wdcn_lo[:, :, :], wdcn_raw[:, :, :], wdcn_hi[:, :, :].bitcast(F32), ALU.subtract).then_inc(wdcn_ready, 1)
            rstd(var1, ve1[:, NT:], rs1[:, NT:], 2, rstd1)

            def product(u, taps=(0, GROUP)):
                b, g = divmod(u, UNITS)
                if b == 0:
                    pool.wait_ge(hats0_ready[1], 1)
                    if u > 0:
                        pool.wait_ge(hats0_ready[0], 1)
                elif g == 0:
                    pool.wait_ge(haty_ready, b)
                if u >= AT_RING:
                    pool.wait_ge(tap_T, GROUP * (u - AT_RING + 1))
                k0, k1 = (g * GROUP + k for k in taps)
                shape = [P, k1 - k0, H, W]
                for j in range(NT):
                    if on_pool(u, j) is True:
                        last = pool.tensor_tensor(
                            at[:, u % AT_RING, j, taps[0]:taps[1], :].rearrange("p k (y x) -> p k y x", x=W),
                            haty[:, b % 2, j, k0:k1, :].unsqueeze(3).broadcast_to(shape),
                            hats[:, b % 2, j, TAPS + k0:TAPS + k1, :].unsqueeze(2).broadcast_to(shape), ALU.mult)
                        last.then_inc(at_pool, 1)

            pool.wait_ge(pos_ready, 1)
            pool.tensor_tensor(dist[:, 1, :, :], pos[:, 0, 1, 0:2 * TAPS].unsqueeze(2).broadcast_to([P, 2 * TAPS, W]),
                               grid[:, :].unsqueeze(1).broadcast_to([P, 2 * TAPS, W]), ALU.subtract).then_inc(dist_ready, 1)
            pool.wait_ge(mask_ready, 1)
            pool.wait_ge(hats_ready, 1)
            pool.tensor_tensor(haty[:, 0, 1, :, :], hats[:, 0, 1, 0:TAPS, :],
                               mask[:, 0, 1, :].unsqueeze(2).broadcast_to([P, TAPS, H]), ALU.mult).then_inc(hats0_ready[1], 1)
            for k in range(GROUP):
                product(0, (k, k + 1))
            pool.iota(eight[:, :], pattern=[[1, E]], base=0, channel_multiplier=0,
                      allow_small_or_imprecise_dtypes=True).then_inc(sel_ready, 1)

            def distances(b):
                pool.wait_ge(pos_ready, b + 1)
                pool.wait_ge(hats_ready, b)
                pool.tensor_tensor(dist[:, :, :, :],
                                   pos[:, b % 2, :, 0:2 * TAPS].unsqueeze(3).broadcast_to([P, NT, 2 * TAPS, W]),
                                   grid[:, :].unsqueeze(1).unsqueeze(1).broadcast_to([P, NT, 2 * TAPS, W]),
                                   ALU.subtract).then_inc(dist_ready, 1)

            def masked_hats(b):
                pool.wait_ge(tanh_done, b + 1)
                pool.tensor_scalar(mask[:, b % 2, :, :], tanh_m[:, b % 2, :, :], 0.5, 0.5, ALU.mult, ALU.add).then_inc(mask_ready, 1)
                pool.wait_ge(mask_ready, b + 1)
                pool.wait_ge(hats_ready, b + 1)
                pool.tensor_tensor(haty[:, b % 2, :, :, :], hats[:, b % 2, :, 0:TAPS, :],
                                   mask[:, b % 2, :, :].unsqueeze(3).broadcast_to([P, NT, TAPS, H]), ALU.mult).then_inc(haty_ready, 1)

            for beat in range(LAST_BEAT + 1):
                for b in due(beat, POOL_AT["haty"], 1):
                    masked_hats(b)
                for b in due(beat, POOL_AT["dist"], 1):
                    distances(b)
                for u in units_due(beat, POOL_AT["product"]):
                    product(u)
                for i in setup_due(beat, "w1_lo"):
                    pool.wait_ge(w1_hi_ready, i + 1)
                    es = slice(i * E // W1_CHUNKS, (i + 1) * E // W1_CHUNKS)
                    pool.tensor_tensor(w1_lo[:, es, :], w1_raw[:, es, :], w1_hi[:, es, :].bitcast(F32), ALU.subtract).then_inc(w1_ready, 1)
                for b in due(beat, POOL_AT["rstd"]):
                    rstd(var2, ve2[:, b % 2, :], rs2[:, b % 2, :], b + 1, rstd2)
                for b, i in second_products(beat):
                    j = i // (2 * HC)
                    if i % (2 * HC) == 2 * HC - 1 and 0 < j < PAIRS - (b == NB - 1):
                        pool.wait_ge(tmp_ready, PAIRS * b + j + 1)
                        if j > 1:
                            pool.wait_ge(ya_ready, (PAIRS - 1) * b + j - 1)
                        elif b > 0:
                            pool.wait_ge(fold_done, b)
                        prev = tmp[:, 0, :] if j == 1 else ya[:, j - 2, :]
                        pool.tensor_tensor(ya[:, j - 1, :], prev, tmp[:, j, :], ALU.add).then_inc(ya_ready, 1)

        @block.scalar
        def _(act):
            for half in range(2):
                act.dma_start(woff_raw[half * C:(half + 1) * C, :, :], w_off).then_inc(ld_woff, 16)
            act.wait_ge(pool_const, 3)
            act.activation(tanh_d[:, 0:1], power[:, 0:1], ACT.Gelu).then_inc(act_chain, 1)
            chain = [1]

            def chained(ins):
                chain[0] += 1
                ins.then_inc(act_chain, 1)
                act.wait_ge(act_chain, chain[0])

            def pad_image(b, bank, col):
                act.wait_ge(xn1T, b + 1)
                act.wait_ge(pool_const, CONSTS)
                act.activation(xpad[:, b, 1:1 + H, 1:1 + W],
                               bank[:, col:col + HW].rearrange("p (y x) -> p y x", x=W), ACT.Copy).then_inc(xpad_ready, 1)
                act.activation(xflat[:, b, :], bank[:, col:col + HW], ACT.Copy).then_inc(xflat_ready, 1)

            def save_offsets(b):
                act.wait_ge(om_done, b + 1)
                bank = bank_h[0] if b == 0 else bank_p
                act.activation(om_sb[:, b % 2, :], bank[0:2 * OM, 0:HW], ACT.Copy).then_inc(om_saved, 1)

            def hat_steps(b):
                act.wait_ge(pos_ready, b + 1)
                act.activation(tanh_m[:, b % 2, :, :], pos[:, b % 2, :, 2 * TAPS:], ACT.Tanh, scale=0.5).then_inc(tanh_done, 1)
                act.wait_ge(dist_ready, b + 1)
                first = NT - 1 if b == 0 else 0
                chained(act.activation(adist[:, first:, :, :], dist[:, first:, :, :], ACT.Abs))
                act.activation(hats[:, b % 2, first:, :, :], adist[:, first:, :, :], ACT.Relu, bias=1.0, scale=-1.0).then_inc(hats_ready, 1)

            def value_hi(b, piece):
                st, k0, n = V_PIECES[piece]
                bank = V0_BANKS[piece] if b == 0 else bank_p
                act.wait_ge(v_done, len(V_PIECES) * b + piece + 1)
                act.activation(v_hl[:, b, st, k0:k0 + n, 0:O], bank[:, 0:n * O].rearrange("p (k o) -> p k o", o=O),
                               ACT.Copy).then_inc(v_hi, 1)

            act.wait_ge(ld_wdcn, 32)
            act.activation(wdcn_hi[:, :, :], wdcn_raw[:, :, :], ACT.Copy).then_inc(wdcn_hi_ready, 1)
            pad_image(0, bank_p, 0)
            save_offsets(0)
            hat_steps(0)
            for piece in range(len(V_PIECES)):
                value_hi(0, piece)
            for beat in range(LAST_BEAT + 1):
                for slot in taps_due(beat, ACT_AT["hi"]):
                    act.wait_ge(tap_T, slot + 1)
                    if slot >= A_RING:
                        act.wait_ge(tap_mm, slot - A_RING + 1)
                    act.activation(a_hi[:, slot % A_RING, :, :].rearrange("p s t -> p (s t)"), t_bank(slot)[:, :],
                                   ACT.Copy).then_inc(tap_hi, 1)
                for b in due(beat, ACT_AT["pad"], 1):
                    pad_image(b, bank_p, 0)
                for i in setup_due(beat, "w1_hi"):
                    act.wait_ge(ld_w1, 32)
                    es = slice(i * E // W1_CHUNKS, (i + 1) * E // W1_CHUNKS)
                    act.activation(w1_hi[:, es, :], w1_raw[:, es, :], ACT.Copy).then_inc(w1_hi_ready, 1)
                if beat == SETUP_AT["sel"]:
                    act.wait_ge(pool_chain, 3)
                    act.activation(sel[:, :, :], sel_f[:, :, :, :].rearrange("r j e o -> r j (e o)"), ACT.Copy).then_inc(sel_ready, 1)
                for b in due(beat, ACT_AT["hats"], 1):
                    hat_steps(b)
                for b in due(beat, ACT_AT["tanh"]):
                    act.wait_ge(diff_ready, b + 1)
                    act.activation(tanh_d[:, :], diff[:, :], ACT.Tanh, scale=0.5).then_inc(tanh_d_done, 1)
                for b in due(beat, ACT_AT["half"]):
                    act.wait_ge(tap_mm, TAPS * (b + 1))
                    if b >= 2:
                        act.wait_ge(t1_ready, b - 1)
                    act.activation(c1[:, b % 2, :], bank_o[O:2 * O, 0:HW], ACT.Copy).then_inc(lo_half, 1)
                for b in due(beat, ACT_AT["conv"], 1):
                    save_offsets(b)
                for b, piece in pieces_due(beat, ACT_AT["value"]):
                    value_hi(b, piece)
                for b in due(beat, ACT_AT["stack"]):
                    act.wait_ge(xn2T, b + 1)
                    if b >= 2:
                        act.wait_ge(h_done, STEPS * (b - 1))
                    act.activation(x2s[:, b % 2, :], bank_c[:, 0:HW], ACT.Copy).then_inc(x2s_ready, 1)
                for b in due(beat, ACT_AT["gate"]):
                    act.wait_ge(lg_done, b + 1)
                    act.activation(lg_sb[:, :], bank_c[0:2 * E, 0:HW], ACT.Copy).then_inc(lg_saved, 1)
                for b in due(beat, ACT_AT["weights"]):
                    act.wait_ge(wdT, b + 1)
                    act.activation(wt[:, :], bank_c[0:2 * E, 0:HW], ACT.Copy).then_inc(wt_ready, 1)
                for half in range(2):
                    for b in due(beat, ACT_AT[f"spread{half}"]):
                        act.wait_ge(spread_done, 2 * b + half + 1)
                        if b >= 2:
                            act.wait_ge(tmp_ready, PAIRS * (b - 1))
                        act.activation(spread[:, b % 2, 2 * half:2 * half + 2, :].rearrange("p j t -> p (j t)"),
                                       bank_c[:, :], ACT.Copy).then_inc(spread_ready, 1)
                for b, i in ffn_steps(beat):
                    n = STEPS * b + i
                    act.wait_ge(h_done, n + 1)
                    if n == 0:
                        act.wait_ge(ld_bias, 48)
                    if n >= H_RING:
                        act.wait_ge(y_done, n - H_RING + 1)
                    act.activation(hid[:, n % H_RING, :], bank_h[n % 2][:, 0:HW], ACT.Gelu, bias=b1_col[:, i:i + 1]).then_inc(h_ready, 1)

        @block.vector
        def _(dve):
            chain = [0]

            def chained(ins):
                chain[0] += 1
                ins.then_inc(dve_chain, 1)
                dve.wait_ge(dve_chain, chain[0])

            def norm_stats(tiles, ready):
                for t in tiles:
                    last = dve.bn_stats(st1[:, t, :], xt[:, t, :])
                chained(last)
                for t in tiles:
                    last = dve.bn_aggr(mv1[:, t, :], st1[:, t, :])
                chained(last)
                a, z = tiles[0], tiles[-1] + 1
                dve.tensor_scalar(ve1[:, a:z], mv1[:, a:z, 1], LN_C_EPS, None, ALU.add).then_inc(ready, 1)

            def norm_apply(tiles, n):
                dve.wait_ge(rstd1, n)
                a, z = tiles[0], tiles[-1] + 1
                whole = [P, z - a, C]
                chained(dve.tensor_tensor(xn1[:, a:z, :], xt[:, a:z, :], mv1[:, a:z, 0:1].broadcast_to(whole), ALU.subtract))
                chained(dve.tensor_tensor(xn1[:, a:z, :], xn1[:, a:z, :], rs1[:, a:z].unsqueeze(2).broadcast_to(whole), ALU.mult))

            def norm_split(tiles):
                a, z = tiles[0], tiles[-1] + 1
                chained(dve.tensor_copy(xn1_hl[:, a:z, 0:C], xn1[:, a:z, :]))
                dve.tensor_tensor(xn1_hl[:, a:z, C:], xn1[:, a:z, :], xn1_hl[:, a:z, 0:C].bitcast(F32),
                                  ALU.subtract).then_inc(xn1_ready, 1)

            def make_base():
                dve.wait_ge(pool_const, 7)
                dve.tensor_scalar(prow_i[:, :], pidx[:, :], 4, None, ALU.arith_shift_right)
                chained(dve.tensor_scalar(pcol_i[:, :], pidx[:, :], W - 1, None, ALU.bitwise_and))
                dve.tensor_copy(prow[:, :], prow_i[:, :])
                chained(dve.tensor_copy(pcol[:, :], pcol_i[:, :]))
                chained(dve.tensor_scalar(tapyx[:, 0:TAPS], tapyx[:, 0:TAPS], prow[:, 0:1], None, ALU.add))
                chained(dve.tensor_scalar(tapyx[:, TAPS:], tapyx[:, TAPS:], pcol[:, 0:1], None, ALU.add))
                for j in range(NT):
                    dve.tensor_scalar(base[:, j, 0:TAPS], tapyx[:, 0:TAPS], float(j * RPT), None, ALU.add)
                    dve.tensor_copy(base[:, j, TAPS:2 * TAPS], tapyx[:, TAPS:])
                    last = dve.memset(base[:, j, 2 * TAPS:], 0.0)
                chained(last)

            def add_bias():
                dve.wait_ge(ld_boff, 16)
                dve.tensor_tensor(base[:, :, :], base[:, :, :], boff_bc[:, :].unsqueeze(1).broadcast_to([P, NT, OM]),
                                  ALU.add).then_inc(base_ready, 1)

            def positions(b):
                dve.wait_ge(omT, b + 1)
                chained(dve.tensor_tensor(pos_a[:, :, :], bank_p[:, 0:NT * 2 * OM].rearrange("p (j m) -> p j m", j=NT)[:, :, 0:OM],
                                          base[:, :, :], ALU.add))
                dve.tensor_tensor(pos[:, b % 2, :, :], bank_p[:, 0:NT * 2 * OM].rearrange("p (j m) -> p j m", j=NT)[:, :, OM:],
                                  pos_a[:, :, :], ALU.add).then_inc(pos_ready, 1)

            def hats_0():
                d, a = dist[:, 0, :, :], adist[:, 0, :, :]
                chained(dve.tensor_tensor(d, pos[:, 0, 0, 0:2 * TAPS].unsqueeze(2).broadcast_to([P, 2 * TAPS, W]),
                                          grid[:, :].unsqueeze(1).broadcast_to([P, 2 * TAPS, W]), ALU.subtract))
                chained(dve.scalar_tensor_tensor(a, d, -1.0, d, ALU.mult, ALU.min))
                dve.tensor_scalar(hats[:, 0, 0, :, :], a, 1.0, 0.0, ALU.add, ALU.max)
                dve.wait_ge(tanh_done, 1)
                dve.tensor_scalar(mask[:, 0, :, :], tanh_m[:, 0, :, :], 0.5, 0.5, ALU.mult, ALU.add).then_inc(mask_ready, 1)
                dve.wait_ge(mask_ready, 1)
                dve.tensor_tensor(haty[:, 0, 0, :, :], hats[:, 0, 0, 0:TAPS, :],
                                  mask[:, 0, 0, :].unsqueeze(2).broadcast_to([P, TAPS, H]), ALU.mult).then_inc(hats0_ready[0], 1)

            def product(u, taps=(0, GROUP)):
                b, g = divmod(u, UNITS)
                if b == 0:
                    dve.wait_ge(hats0_ready[0], 1)
                    if u > 0:
                        dve.wait_ge(hats0_ready[1], 1)
                elif g == 0:
                    dve.wait_ge(haty_ready, b)
                if u >= AT_RING:
                    dve.wait_ge(tap_T, GROUP * (u - AT_RING + 1))
                k0, k1 = (g * GROUP + k for k in taps)
                shape = [P, k1 - k0, H, W]
                for j in range(NT):
                    if on_pool(u, j) is False:
                        last = dve.tensor_tensor(
                            at[:, u % AT_RING, j, taps[0]:taps[1], :].rearrange("p k (y x) -> p k y x", x=W),
                            haty[:, b % 2, j, k0:k1, :].unsqueeze(3).broadcast_to(shape),
                            hats[:, b % 2, j, TAPS + k0:TAPS + k1, :].unsqueeze(2).broadcast_to(shape), ALU.mult)
                        last.then_inc(at_dve, 1)

            def value_lo(b, piece):
                st, k0, n = V_PIECES[piece]
                bank = V0_BANKS[piece] if b == 0 else bank_p
                dve.wait_ge(v_hi, len(V_PIECES) * b + piece + 1)
                dve.tensor_tensor(v_hl[:, b, st, k0:k0 + n, O:], bank[:, 0:n * O].rearrange("p (k o) -> p k o", o=O),
                                  v_hl[:, b, st, k0:k0 + n, 0:O].bitcast(F32), ALU.subtract).then_inc(v_lo, 1)

            def split(hi, lo, raw, ready):
                chained(dve.tensor_copy(hi, raw))
                dve.tensor_tensor(lo, raw, hi.bitcast(F32), ALU.subtract).then_inc(ready, 1)

            first, rest = list(range(NT)), list(range(NT, NB * NT))
            make_base()
            dve.wait_ge(ld_xt0, 16)
            norm_stats(first, var1)
            add_bias()
            norm_apply(first, 1)
            norm_split(first)
            dve.wait_ge(ld_woff, 32)
            split(woff[:, :, 0:OM], woff[:, :, OM:], woff_raw[:, :, :], woff_ready)
            dve.wait_ge(ld_xt1, 16)
            norm_stats(rest, var1)
            dve.wait_ge(ld_wg, 32)
            split(wg_hl[:, 0:E], wg_hl[:, E:], wg_raw[:, :], wg_ready)
            dve.tensor_copy(fold[0:O, :], ident[0:O, 0:O])
            dve.tensor_copy(fold[O:, :], ident[O:, O:]).then_inc(fold_ready, 1)
            dve.wait_ge(base_ready, 1)
            positions(0)
            dve.wait_ge(pos_ready, 1)
            hats_0()
            product(0, (0, 1))
            for k in range(1, GROUP):
                product(0, (k, k + 1))

            for beat in range(LAST_BEAT + 1):
                for b in due(beat, DVE_AT["xn"], 1):
                    norm_apply([NT * b, NT * b + 1], 2)
                    norm_split([NT * b, NT * b + 1])
                for b in due(beat, DVE_AT["positions"], 1):
                    positions(b)
                for b, piece in pieces_due(beat, DVE_AT["value"]):
                    value_lo(b, piece)
                for u in units_due(beat, DVE_AT["product"]):
                    product(u)
                for slot in taps_due(beat, DVE_AT["lo"]):
                    dve.wait_ge(tap_hi, slot + 1)
                    dve.tensor_tensor(a_lo[:, slot % A_RING, :, :].rearrange("p s t -> p (s t)"), t_bank(slot)[:, :],
                                      a_hi[:, slot % A_RING, :, :].bitcast(F32).rearrange("p s t -> p (s t)"),
                                      ALU.subtract).then_inc(tap_lo, 1)
                for piece in setup_due(beat, "v0_"):
                    value_lo(0, piece)
                for b in due(beat, DVE_AT["residual"]):
                    if b == 0:
                        dve.wait_ge(ld_xc, 16)
                    dve.wait_ge(lo_half, b + 1)
                    chained(dve.tensor_tensor(c2[:, b % 2, :], c1[:, b % 2, :], xc[:, b, :], ALU.add))
                    dve.tensor_tensor(t1[:, b, :], bank_o[0:O, 0:HW], c2[:, b % 2, :], ALU.add).then_inc(t1_ready, 1)
                for b in due(beat, DVE_AT["stats"]):
                    dve.wait_ge(t1T, b + 1)
                    for j in range(NT):
                        last = dve.bn_stats(st2[:, j, :], bank_c[:, j * O:(j + 1) * O])
                    chained(last)
                    for j in range(NT):
                        last = dve.bn_aggr(mv2[:, b % 2, j, :], st2[:, j, :])
                    chained(last)
                    dve.tensor_scalar(ve2[:, b % 2, :], mv2[:, b % 2, :, 1], LN_T_EPS, None, ALU.add).then_inc(var2, 1)
                for b in due(beat, DVE_AT["norm"]):
                    dve.wait_ge(rstd2, b + 1)
                    for j in range(NT):
                        last = dve.tensor_scalar(xn2[:, j, :], bank_c[:, j * O:(j + 1) * O], mv2[:, b % 2, j, 0:1],
                                                 rs2[:, b % 2, j:j + 1], ALU.subtract, ALU.mult)
                    chained(last)
                    if b > 0:
                        dve.wait_ge(xn2T, b)
                    split(xn2_hl[:, :, 0:C], xn2_hl[:, :, C:], xn2[:, :, :], xn2_ready)
                for b in due(beat, DVE_AT["top"]):
                    dve.wait_ge(lgT, b + 1)
                    if b == 0:
                        dve.wait_ge(ld_bias, 48)
                    lg = bank_c[:, 0:NT * 2 * E].rearrange("p (j m) -> p j m", j=NT)
                    chained(dve.tensor_tensor(lg_a[:, :, :], lg[:, :, 0:E],
                                              bg_bc[:, :].unsqueeze(1).broadcast_to([P, NT, E]), ALU.add))
                    dve.tensor_tensor(logit[:, :, :], lg[:, :, E:], lg_a[:, :, :], ALU.add).then_inc(logit_ready, 1)
                    dve.wait_ge(logit_ready, b + 1)
                    for j in range(NT):
                        last = dve.max(top[:, j, :], logit[:, j, :])
                    chained(last)
                    dve.tensor_tensor(diff[:, :], top[:, :, 0], top[:, :, 1], ALU.subtract).then_inc(diff_ready, 1)
                    for j in range(NT):
                        last = dve.max_index(topi[:, j, :], top[:, j, :], logit[:, j, :])
                    chained(last)
                    chained(dve.tensor_copy(topf[:, :, :], topi[:, :, 0:2]))
                    if b == 0:
                        dve.wait_ge(sel_ready, 1)
                    dve.tensor_tensor(onehot[:, :, :, :], eight[:, :].unsqueeze(1).unsqueeze(1).broadcast_to([P, NT, 2, E]),
                                      topf[:, :, :].unsqueeze(3).broadcast_to([P, NT, 2, E]), ALU.is_equal)
                for b in due(beat, DVE_AT["gates"]):
                    dve.wait_ge(tanh_d_done, b + 1)
                    dve.tensor_scalar(pw[:, :, 0], tanh_d[:, :], 0.5, 0.5, ALU.mult, ALU.add)
                    chained(dve.tensor_scalar(pw[:, :, 1], tanh_d[:, :], -0.5, 0.5, ALU.mult, ALU.add))
                    chained(dve.tensor_tensor(gated[:, :, :, :], onehot[:, :, :, :],
                                              pw[:, :, :].unsqueeze(3).broadcast_to([P, NT, 2, E]), ALU.mult))
                    chained(dve.tensor_tensor(wd[:, :, :], gated[:, :, 0, :], gated[:, :, 1, :], ALU.add))
                    split(wd_hl[:, :, 0:E], wd_hl[:, :, E:], wd[:, :, :], wd_ready)
                for b, i in second_products(beat):
                    if i % (2 * HC) == 2 * HC - 1:
                        j = i // (2 * HC)
                        dve.wait_ge(y_done, STEPS * b + i + 1)
                        dve.wait_ge(spread_ready, 2 * b + j // 2 + 1)
                        if b > 0:
                            dve.wait_ge(ya_ready, (PAIRS - 1) * (b - 1) + max(j, 1))
                        dve.scalar_tensor_tensor(tmp[:, j, :], Y_BANKS[b][j][:, 0:HW], b2_col[:, j:j + 1], spread[:, b % 2, j, :],
                                                 ALU.add, ALU.mult).then_inc(tmp_ready, 1)
                    if i == STEPS - 1:
                        dve.wait_ge(fold_done, b + 1)
                        dve.tensor_tensor(fin[:, b, :], bank_c[0:O, 0:HW], t1[:, b, :], ALU.add).then_inc(fin_ready, 1)

        @block.tensor
        def _(pe):
            released = {}

            def take(name, sem_, value):
                if name in released:
                    pe.wait_ge(*released[name])
                released[name] = (sem_, value)

            def transpose_xn(b, bank, col):
                pe.wait_ge(xn1_ready, b + 1)
                for j in range(NT):
                    last = pe.transpose(bank[:, col + j * P:col + (j + 1) * P], xn1_hl[:, NT * b + j, :].bitcast(F32), ident[:, :])
                last.then_inc(xn1T, 1)

            def conv(b):
                bank = bank_h[0] if b == 0 else bank_p
                if b > 0:
                    take("p", om_saved, b + 1)
                pe.wait_ge(xpad_ready, b + 1)
                for k in range(TAPS):
                    ky, kx = divmod(k, KS)
                    last = pe.matmul(bank[0:2 * OM, 0:HW], woff[:, k, :], xpad[:, b, ky:ky + H, kx:kx + W],
                                     start=(k == 0), stop=(k == TAPS - 1))
                last.then_inc(om_done, 1)

            def transpose_om(b):
                take("p", pos_ready, b + 1)
                for j in range(NT):
                    last = pe.transpose(bank_p[:, j * 2 * OM:(j + 1) * 2 * OM], om_sb[:, b % 2, j * P:(j + 1) * P],
                                        ident[0:2 * OM, 0:2 * OM])
                last.then_inc(omT, 1)

            def value(b, piece):
                st, k0, n = V_PIECES[piece]
                count = len(V_PIECES) * b + piece + 1
                if b == 0:
                    bank = V0_BANKS[piece]
                    released[("c", "y", "o", "h1")[piece]] = (v_lo, count)
                else:
                    bank = bank_p
                    take("p", v_lo, count)
                pe.wait_ge(wdcn_ready, 1)
                pe.wait_ge(xflat_ready, b + 1)
                src = xflat[:, b, st * P:(st + 1) * P]
                pe.matmul(bank[:, 0:n * O], src, wdcn_hi[:, k0:k0 + n, :], start=True, stop=False)
                pe.matmul(bank[:, 0:n * O], src, wdcn_lo[:, k0:k0 + n, :], start=False, stop=True).then_inc(v_done, 1)

            pe.wait_ge(pool_const, 2)
            for _ in range(WARM):
                pe.matmul(bank_y[:, 0:P], ident[:, :], ident[:, :], start=True, stop=True)
            released["p"] = (xflat_ready, 1)
            transpose_xn(0, bank_p, 0)
            pe.wait_ge(woff_ready, 1)
            conv(0)
            pe.wait_ge(om_saved, 1)
            transpose_om(0)
            for piece in range(len(V_PIECES)):
                value(0, piece)
            def sample(slot):
                b, k = divmod(slot, TAPS)
                pe.wait_ge(tap_lo, slot + 1)
                if k == 0:
                    pe.wait_ge(v_lo, len(V_PIECES) * (b + 1))
                    if b > 0:
                        pe.wait_ge(t1_ready, b)
                for st in range(ST):
                    for part in (a_hi, a_lo):
                        last = pe.matmul(bank_o[:, 0:HW], v_hl[:, b, st, k, :], part[:, slot % A_RING, st, :],
                                         start=(k == 0 and st == 0 and part is a_hi),
                                         stop=(k == TAPS - 1 and st == ST - 1 and part is a_lo))
                last.then_inc(tap_mm, 1)

            def hidden(b, i):
                n = STEPS * b + i
                e, c = divmod(i, HC)
                if n == 0:
                    pe.wait_ge(tap_lo, T_WIDE)
                if b == 0 and i % (STEPS // W1_CHUNKS) == 0:
                    pe.wait_ge(w1_ready, i // (STEPS // W1_CHUNKS) + 1)
                if i == 0:
                    pe.wait_ge(x2s_ready, b + 1)
                if n >= 2:
                    pe.wait_ge(h_ready, n - 1)
                pe.matmul(bank_h[n % 2][:, 0:HW], w1_hi[:, e, c * P:(c + 1) * P], x2s[:, b % 2, :], start=True, stop=False)
                pe.matmul(bank_h[n % 2][:, 0:HW], w1_lo[:, e, c * P:(c + 1) * P], x2s[:, b % 2, :], start=False, stop=True).then_inc(h_done, 1)

            def expert_out(n):
                b, i = divmod(n, STEPS)
                e, c = divmod(i, HC)
                if n == 0:
                    pe.wait_ge(ld_w2, 16)
                j = i // (2 * HC)
                if i % (2 * HC) == 0 and (b < NB - 1 or j == 0):
                    take("y", tmp_ready, PAIRS * b + j + 1)
                if b == NB - 1 and i == 2 * HC:
                    pe.wait_ge(v_lo, len(V_PIECES) * NB)
                    pe.wait_ge(tap_lo, SLOTS)
                pe.wait_ge(h_ready, n + 1)
                half = O * (e % 2)
                pe.matmul(Y_BANKS[b][j][half:half + O, 0:HW], w2_sb[:, e, c, :], hid[:, n % H_RING, :],
                          start=(c == 0), stop=(c == HC - 1)).then_inc(y_done, 1)
                if i == STEPS - 1:
                    take("c", fin_ready, b + 1)
                    pe.wait_ge(fold_ready, 1)
                    last_b = b == NB - 1
                    pe.wait_ge(ya_ready, (PAIRS - 1) * (b + 1) - last_b)
                    last = pe.matmul(bank_c[0:O, 0:HW], fold[:, :], ya[:, PAIRS - 2 - last_b, :], start=True, stop=not last_b)
                    if last_b:
                        pe.wait_ge(tmp_ready, PAIRS * NB)
                        last = pe.matmul(bank_c[0:O, 0:HW], fold[:, :], tmp[:, PAIRS - 1, :], start=False, stop=True)
                    last.then_inc(fold_done, 1)

            pending = []
            for beat in range(LAST_BEAT + 1):
                for slot in taps_due(beat, PE_AT["tap"]):
                    pe.wait_ge(at_dve, made(slot, False))
                    pe.wait_ge(at_pool, made(slot, True))
                    last_tap = max((t for t in range(slot) if t_bank(t) is t_bank(slot)), default=None)
                    if last_tap is not None:
                        pe.wait_ge(tap_lo, last_tap + 1)
                    if slot == 3:
                        pe.wait_ge(v_lo, len(V_PIECES))
                    for st in range(ST):
                        for j in range(NT):
                            last = pe.transpose(t_bank(slot)[:, st * HW + j * P:st * HW + (j + 1) * P],
                                                at[:, slot // GROUP % AT_RING, j, slot % GROUP, st * P:(st + 1) * P], ident[:, :])
                    last.then_inc(tap_T, 1)
                for slot in taps_due(beat, PE_AT["sample"]):
                    sample(slot)
                for b in due(beat, PE_AT["xn"], 1):
                    take("p", xflat_ready, b + 1)
                    transpose_xn(b, bank_p, 0)
                for b in due(beat, PE_AT["conv"], 1):
                    conv(b)
                for b in due(beat, PE_AT["om"], 1):
                    pe.wait_ge(om_saved, b + 1)
                    transpose_om(b)
                for b, piece in pieces_due(beat, PE_AT["value"]):
                    value(b, piece)
                for b in due(beat, PE_AT["t1"]):
                    take("c", xn2_ready, b + 1)
                    pe.wait_ge(t1_ready, b + 1)
                    for j in range(NT):
                        last = pe.transpose(bank_c[:, j * O:(j + 1) * O], t1[:, b, j * P:(j + 1) * P], ident[0:O, 0:O])
                    last.then_inc(t1T, 1)
                for b in due(beat, PE_AT["stack"]):
                    take("c", x2s_ready, b + 1)
                    pe.wait_ge(xn2_ready, b + 1)
                    for j in range(NT):
                        last = pe.transpose(bank_c[:, j * P:(j + 1) * P], xn2_hl[:, j, :].bitcast(F32), ident[:, :])
                    last.then_inc(xn2T, 1)
                for b in due(beat, PE_AT["gate"]):
                    take("c", lg_saved, b + 1)
                    pe.wait_ge(wg_ready, 1)
                    pe.wait_ge(x2s_ready, b + 1)
                    pe.matmul(bank_c[0:2 * E, 0:HW], wg_hl[:, :], x2s[:, b % 2, :], start=True, stop=True).then_inc(lg_done, 1)
                for b in due(beat, PE_AT["logits"]):
                    pe.wait_ge(lg_saved, b + 1)
                    take("c", logit_ready, b + 1)
                    for j in range(NT):
                        last = pe.transpose(bank_c[:, j * 2 * E:(j + 1) * 2 * E], lg_sb[:, j * P:(j + 1) * P], ident[0:2 * E, 0:2 * E])
                    last.then_inc(lgT, 1)
                for b in due(beat, PE_AT["weights"]):
                    take("c", wt_ready, b + 1)
                    pe.wait_ge(wd_ready, b + 1)
                    for j in range(NT):
                        last = pe.transpose(bank_c[0:2 * E, j * P:(j + 1) * P], wd_hl[:, j, :].bitcast(F32), ident[:, :])
                    last.then_inc(wdT, 1)
                for half in range(2):
                    for b in due(beat, PE_AT[f"spread{half}"]):
                        take("c", spread_ready, 2 * b + half + 1)
                        pe.wait_ge(wt_ready, b + 1)
                        pe.wait_ge(sel_ready, 2)
                        for j in range(2):
                            last = pe.matmul(bank_c[:, j * HW:(j + 1) * HW], sel[:, 2 * half + j, :], wt[:, :], start=True, stop=True)
                        last.then_inc(spread_done, 1)
                for b, i in ffn_steps(beat):
                    hidden(b, i)
                    pending.append(STEPS * b + i)
                    if len(pending) > LAG:
                        expert_out(pending.pop(0))
            while pending:
                expert_out(pending.pop(0))


def kernel(**inputs):
    import numpy as np
    import concourse.bacc as bacc
    from concourse.bass_utils import run_bass_kernel_spmd

    x = np.asarray(inputs["x"])
    w_off = np.asarray(inputs["L0_conv_w_off"])
    b_off = np.asarray(inputs["L0_conv_b_off"])
    order = np.concatenate([np.arange(TAPS) * 2, np.arange(TAPS) * 2 + 1, np.arange(2 * TAPS, 3 * TAPS)])
    arrays = {
        "x_tok": x.reshape(NB, C, NT, P).transpose(3, 0, 2, 1).reshape(P, NB * NT, C),
        "x_ch": x.reshape(NB, C, HW).transpose(1, 0, 2),
        "w_off": w_off[order].reshape(OM, C, TAPS).transpose(1, 2, 0),
        "b_off": b_off[order],
        "w_dcn": np.asarray(inputs["L0_conv_w_dcn"]).reshape(O, C, TAPS).transpose(1, 2, 0),
        "wg": np.asarray(inputs["L0_ffn_Wg"]),
        "bg": np.asarray(inputs["L0_ffn_bg"]),
        "w1": np.asarray(inputs["L0_ffn_W1"]).transpose(1, 0, 2),
        "b1": np.asarray(inputs["L0_ffn_b1"]).reshape(STEPS, P).T,
        "w2": np.asarray(inputs["L0_ffn_W2"]).reshape(E, HC, P, O).transpose(2, 0, 1, 3),
        "b2": np.asarray(inputs["L0_ffn_b2"]).reshape(PAIRS, 2 * O).T,
    }
    arrays = {f"in_{n}": np.ascontiguousarray(a) for n, a in arrays.items()}
    nc = bacc.Bacc("TRN2", target_bir_lowering=False, num_devices=1)
    args = [nc.dram_tensor(n, a.shape, mybir.dt.from_np(a.dtype), kind="ExternalInput").ap() for n, a in arrays.items()]
    out = nc.dram_tensor("out_0", (NB, C, HW), F32, kind="ExternalOutput").ap()
    metaformer_kernel(nc, *args, out)
    r = run_bass_kernel_spmd(nc, [arrays], core_ids=[0])
    return r.results[0]["out_0"].reshape(NB, C, H, W)
```

```python
from contextlib import ExitStack

import concourse.bass as bass
from concourse import mybir

F32 = mybir.dt.float32
F32R = mybir.dt.float32r
I32 = mybir.dt.int32
U32 = mybir.dt.uint32
ACT = mybir.ActivationFunctionType
ALU = mybir.AluOpType

P = 128
NB, C, H, W = 4, 64, 16, 16
HW = H * W
NT = HW // P
KS = 3
TAPS = KS * KS
OM = 3 * TAPS
O = 64
E, HID = 8, 256
HC = HID // P
PAIRS = E // 2
ST = HW // P
RPT = P // W
HP, WP = H + 2, W + 2
GROUP = 3
UNITS = TAPS // GROUP
SLOTS = NB * TAPS
TAP_BEATS = 4
BEATS = TAP_BEATS * TAPS
W1_CHUNKS = 2
V_PIECES = [(st, lo, n) for st in range(ST) for lo, n in ((0, 5), (5, 4))]
LN_C_EPS, LN_T_EPS = 1e-6, 1e-5
AT_RING, A_RING, H_RING = 4, 6, 3
T_WIDE = 12
LAG = 1
WARM = 10
WARM_TAPS = 8


PE_AT = dict(tap=0, sample=8, conv=(-27, -32, -31, -32), om=(-23, -28, -27, -28), value=(-15, -21, -17, -17),
             t1=(43, 47, 47, 51), stack=(54, 54, 54, 58), gate=(58, 59, 58, 62), logits=(60, 66, 60, 64),
             weights=(70, 71, 70, 76), spread0=(74, 74, 74, 81), spread1=(77, 78, 81, 83), xn=(-31, -33, -34, -33),
             fold=(110, 110, 114, 97))
ACT_AT = dict(hi=0, hats=(-11, -20, -20, -20), conv=(-26, -30, -30, -31), value=(-17, -23, -17, -19),
              half=(37, 39, 40, 40), stack=(54, 54, 54, 58), gate=(58, 56, 56, 61), tanh=(64, 66, 64, 70),
              weights=(69, 70, 70, 75), spread0=(73, 74, 74, 79), spread1=(77, 79, 78, 83), pad=(-42, -34, -35, -34))
DVE_AT = dict(lo=4, positions=(-18, -24, -24, -24), value=(-13, -19, -14, -15),
              product=(0, 0, 0, -12, -13, -14, -12, -13, -14, -12, -13, -14, -6, -7, -8, -6, -7, -8, -12, -13, -14,
                  -7, -14, -15, -13, -8, -9, -9, -3, -10, -7, -8, -9, -7, -8, -13), residual=(41, 41, 40, 41),
              stats=(46, 44, 44, 48), norm=(48, 51, 51, 55), top=(60, 64, 64, 68), gates=(64, 66, 66, 70),
              xn=(-34, -36, -39, -36), fin=(111, 111, 111, 98), spread0=(75, 75, 75, 79), spread1=(79, 79, 79, 83))
POOL_AT = dict(dist=(-19, -28, -28, -28), haty=(-12, -19, -19, -15), product=(3, 5, 3, 3, 3, 3, 3, 3, 3, 3, 3, -1),
               rstd=(42, 41, 40, 45))
SETUP_AT = dict(w1_hi0=11, w1_hi1=29, w1_lo0=40, w1_lo1=41, sel=31, v0_0=3, v0_1=6, v0_2=1, v0_3=1)
VALUE_STEP = 6
FFN_AT = [[67, 74, 77, 83, 88, 93, 97, 105],
          [69, 74, 77, 83, 88, 98, 100, 104],
          [71, 74, 85, 89, 91, 92, 97, 106],
          [74, 77, 80, 81, 82, 86, 89, 89]]
POOL_TILES = [(1,), (0, 1), (1,), (0, 1), (0, 1), (1,), (0, 1), (0, 1), (0, 1), (0, 1), (0, 1), (0, 1)]
W1_POOL = [True, False]
LAST_BEAT = BEATS * (NB - 1) + FFN_AT[-1][-1]


def due(beat, offset, first=0):
    offsets = (offset,) * NB if isinstance(offset, int) else offset
    return [b for b in range(first, NB) if BEATS * b + offsets[b] == beat]


def setup_due(beat, name):
    return [i for i in range(len(V_PIECES)) if SETUP_AT.get(f"{name}{i}") == beat]


def taps_due(beat, offset):
    slot, rest = divmod(beat - offset, TAP_BEATS)
    return [slot] if rest == 0 and 0 <= slot < SLOTS else []


def pieces_due(beat, offset):
    offsets = (offset,) * NB if isinstance(offset, int) else offset
    return [(b, piece) for b in range(1, NB) for piece in range(len(V_PIECES))
            if BEATS * b + offsets[b] + VALUE_STEP * piece == beat]


def units_due(beat, offset):
    offsets = (offset,) * NB * UNITS if isinstance(offset, int) else offset
    return [u for u in range(1, NB * UNITS) if TAP_BEATS * GROUP * (u - 1) + offsets[u] == beat]


def products_due(beat, offset):
    offsets = (offset,) * SLOTS if isinstance(offset, int) else offset
    return [slot for slot in range(GROUP, SLOTS) if TAP_BEATS * slot + offsets[slot] == beat]


def on_pool(u, j):
    return j in POOL_TILES[u]


def made(slot, pool):
    if slot < GROUP:
        return slot + 1
    if pool:
        return GROUP + sum(on_pool(u, j) for u in range(1, slot // GROUP + 1) for j in range(NT))
    return GROUP + sum(not on_pool(t // GROUP, j) for t in range(GROUP, slot + 1) for j in range(NT))


def first_products(beat):
    return [(b, e) for b in range(NB) for e in range(E) if BEATS * b + FFN_AT[b][e] == beat]


def second_products(beat):
    def through(s):
        first = sum(BEATS * b + FFN_AT[b][e] <= s for b in range(NB) for e in range(E))
        return first if s == LAST_BEAT else max(0, first - LAG)
    return [divmod(n, E) for n in range(through(beat - 1), through(beat))]


def metaformer_kernel(nc, x_tok, x_ch, w_off, b_off, w_dcn, wg, bg, w1, b1, w2, b2, out):
    ctx = ExitStack()
    with ctx:
        def sb(name, shape, dt=F32):
            return ctx.enter_context(nc.sbuf_tensor(name, shape, dt))

        def ps(name):
            return ctx.enter_context(nc.psum_tensor(name, [P, 512], F32))

        def sem(name):
            return ctx.enter_context(nc.semaphore(name))

        xt = sb("xt", [P, NB * NT, C])
        xc = sb("xc", [C, NB, HW])
        woff_raw = sb("woff_raw", [P, TAPS, OM])
        wdcn_raw = sb("wdcn_raw", [P, TAPS, O])
        w1_raw = sb("w1_raw", [P, E // 2, HID])
        w1_half_hi = sb("w1_half_hi", [P, E // 2, HID], F32R)
        w1_half_lo = sb("w1_half_lo", [P, E // 2, HID], F32R)
        wg_raw = sb("wg_raw", [P, E])
        boff_bc = sb("boff_bc", [P, OM])
        bg_bc = sb("bg_bc", [P, E])
        b1_col = sb("b1_col", [P, E * HC])
        b2_col = sb("b2_col", [P, PAIRS])
        w2_sb = sb("w2_sb", [P, E, HC, O])
        woff = sb("woff", [P, TAPS, 2 * OM], F32R)
        wdcn_hi = sb("wdcn_hi", [P, TAPS, O], F32R)
        wdcn_lo = sb("wdcn_lo", [P, TAPS, O], F32R)
        w1_hi = sb("w1_hi", [P, E, HID], F32R)
        w1_lo = sb("w1_lo", [P, E, HID], F32R)
        wg_hl = sb("wg_hl", [P, 2 * E], F32R)
        ident = sb("ident", [P, P])
        fold = sb("fold", [P, O])
        sel_f = sb("sel_f", [2 * E, PAIRS, 2, O])
        sel = sb("sel", [2 * E, PAIRS, 2 * O], F32R)
        grid = sb("grid", [P, W])
        eight = sb("eight", [P, E])
        power = sb("power", [P, NB * NT])
        pidx = sb("pidx", [P, 1], I32)
        prow_i = sb("prow_i", [P, 1], I32)
        pcol_i = sb("pcol_i", [P, 1], I32)
        prow = sb("prow", [P, 1])
        pcol = sb("pcol", [P, 1])
        tapyx = sb("tapyx", [P, 2 * TAPS])
        base = sb("base", [P, NT, OM])
        st1 = sb("st1", [P, NB * NT, 6])
        mv1 = sb("mv1", [P, NB * NT, 2])
        ve1 = sb("ve1", [P, NB * NT])
        rs1 = sb("rs1", [P, NB * NT])
        xn1 = sb("xn1", [P, NB * NT, C])
        xn1_hl = sb("xn1_hl", [P, NB * NT, 2 * C], F32R)
        xpad = sb("xpad", [P, NB, HP, WP], F32R)
        xflat = sb("xflat", [P, NB, HW], F32R)
        om_sb = sb("om_sb", [2 * OM, 2, HW])
        pos_a = sb("pos_a", [P, NT, OM])
        pos = sb("pos", [P, 2, NT, OM])
        tanh_m = sb("tanh_m", [P, 2, NT, TAPS])
        mask = sb("mask", [P, 2, NT, TAPS])
        dist = sb("dist", [P, NT, 2 * TAPS, W])
        adist = sb("adist", [P, NT, 2 * TAPS, W])
        hats = sb("hats", [P, 2, NT, 2 * TAPS, W])
        haty = sb("haty", [P, 2, NT, TAPS, W])
        at = sb("at", [P, AT_RING, NT, GROUP, HW])
        a_hi = sb("a_hi", [P, A_RING, ST, HW], F32R)
        a_lo = sb("a_lo", [P, A_RING, ST, HW], F32R)
        v_hl = sb("v_hl", [P, NB, ST, TAPS, 2 * O], F32R)
        c1 = sb("c1", [O, 2, HW])
        c2 = sb("c2", [O, 2, HW])
        t1 = sb("t1", [O, NB, HW])
        st2 = sb("st2", [P, NT, 6])
        mv2 = sb("mv2", [P, 2, NT, 2])
        ve2 = sb("ve2", [P, 2, NT])
        rs2 = sb("rs2", [P, 2, NT])
        xn2 = sb("xn2", [P, NT, C])
        xn2_hl = sb("xn2_hl", [P, NT, 2 * C], F32R)
        x2s = sb("x2s", [P, 2, HW], F32R)
        lg_sb = sb("lg_sb", [2 * E, HW])
        lg_a = sb("lg_a", [P, NT, E])
        logit = sb("logit", [P, NT, E])
        top = sb("top", [P, NT, 8])
        topi = sb("topi", [P, NT, 8], U32)
        topf = sb("topf", [P, NT, 2])
        diff = sb("diff", [P, NT])
        tanh_d = sb("tanh_d", [P, NT])
        pw = sb("pw", [P, NT, 2])
        onehot = sb("onehot", [P, NT, 2, E])
        gated = sb("gated", [P, NT, 2, E])
        wd = sb("wd", [P, NT, E])
        wd_hl = sb("wd_hl", [P, NT, 2 * E], F32R)
        wt = sb("wt", [2 * E, HW], F32R)
        spread = sb("spread", [P, 2, PAIRS, HW])
        hid = sb("hid", [P, H_RING, HC, HW])
        tmp = sb("tmp", [P, PAIRS, HW])
        ya = sb("ya", [P, 3, HW])
        fin = sb("fin", [O, NB, HW])

        bank_t = [ps("bank_t0"), ps("bank_t1")]
        bank_o = ps("bank_o")
        bank_p = ps("bank_p")
        bank_c = ps("bank_c")
        bank_h = [ps("bank_h0"), ps("bank_h1")]
        bank_y = ps("bank_y")
        Y_BANKS = [[bank_y] * PAIRS] * (NB - 2) + [[bank_y, bank_p] * 2, [bank_y, bank_p, *bank_t]]

        def h_bank(n):
            return bank_h[n % 2] if n < E * (NB - 1) else [*bank_h, bank_o][n % 3]

        def t_bank(slot):
            return (bank_t + bank_h)[slot % 4] if slot < T_WIDE else bank_t[slot % 2]

        V0_BANKS = [bank_c, bank_y, bank_o, bank_h[1]]

        ld_xt0, ld_xt1, ld_xc, ld_woff, ld_wdcn = (sem(n) for n in ("ld_xt0", "ld_xt1", "ld_xc", "ld_woff", "ld_wdcn"))
        ld_w1, ld_w2, ld_wg, ld_boff, ld_bias = (sem(n) for n in ("ld_w1", "ld_w2", "ld_wg", "ld_boff", "ld_bias"))
        pool_const = sem("pool_const")
        base_ready, woff_ready, wdcn_ready, wg_ready, w1_lo_ready, w1_copied, fold_ready, sel_ready, eight_ready = (
            sem(n) for n in ("base_ready", "woff_ready", "wdcn_ready", "wg_ready", "w1_lo_ready", "w1_copied", "fold_ready", "sel_ready", "eight_ready"))
        hats0_ready = [sem("hats0_ready0"), sem("hats0_ready1")]
        wdcn_hi_ready, w1_hi_ready, mask_ready = sem("wdcn_hi_ready"), sem("w1_hi_ready"), sem("mask_ready")
        dve_chain, act_chain, pool_chain = sem("dve_chain"), sem("act_chain"), sem("pool_chain")
        var1, rstd1, xn1_ready, xn1T, xpad_ready, xflat_ready = (
            sem(n) for n in ("var1", "rstd1", "xn1_ready", "xn1T", "xpad_ready", "xflat_ready"))
        om_done, om_saved, omT, pos_ready, tanh_done, dist_ready, hats_ready, haty_ready = (
            sem(n) for n in ("om_done", "om_saved", "omT", "pos_ready", "tanh_done", "dist_ready", "hats_ready", "haty_ready"))
        v_done, v_hi, v_lo = sem("v_done"), sem("v_hi"), sem("v_lo")
        at_dve, at_pool = sem("at_dve"), sem("at_pool")
        tap_T, tap_hi, tap_lo, tap_mm = sem("tap_T"), sem("tap_hi"), sem("tap_lo"), sem("tap_mm")
        lo_half, t1_ready, t1T, var2, rstd2, xn2_ready, xn2T, x2s_ready = (
            sem(n) for n in ("lo_half", "t1_ready", "t1T", "var2", "rstd2", "xn2_ready", "xn2T", "x2s_ready"))
        lg_done, lg_saved, lgT, logit_ready, diff_ready, tanh_d_done, wd_ready, wdT, wt_ready, spread_done, spread_ready = (
            sem(n) for n in ("lg_done", "lg_saved", "lgT", "logit_ready", "diff_ready", "tanh_d_done", "wd_ready", "wdT", "wt_ready",
                             "spread_done", "spread_ready"))
        h_done, h_ready, y_done, tmp_ready, ya_ready, fold_done, fin_ready, stored = (
            sem(n) for n in ("h_done", "h_ready", "y_done", "tmp_ready", "ya_ready", "fold_done", "fin_ready", "stored"))
        CONSTS = 8

        block = ctx.enter_context(nc.Block())

        @block.sync
        def _(sp):
            sp.dma_start(xt[:, 0:NT, :], x_tok[:, 0:NT, :]).then_inc(ld_xt0, 16)
            sp.dma_start(xt[:, NT:, :], x_tok[:, NT:, :]).then_inc(ld_xt1, 16)
            sp.dma_start(boff_bc[:, :], b_off.partition_broadcast(P)).then_inc(ld_boff, 16)
            for half in range(2):
                sp.dma_start(wdcn_raw[half * C:(half + 1) * C, :, :], w_dcn).then_inc(ld_wdcn, 16)
            for half in range(2):
                sp.dma_start(wg_raw[half * C:(half + 1) * C, :], wg).then_inc(ld_wg, 16)
            sp.dma_start(w1_raw[:, :, :], w1).then_inc(ld_w1, 16)
            sp.dma_start(xc[:, :, :], x_ch).then_inc(ld_xc, 16)
            sp.dma_start(bg_bc[:, :], bg.partition_broadcast(P)).then_inc(ld_bias, 16)
            sp.dma_start(b1_col[:, :], b1).then_inc(ld_bias, 16)
            sp.dma_start(b2_col[:, :], b2).then_inc(ld_bias, 16)
            sp.dma_start(w2_sb[:, :, :, :], w2).then_inc(ld_w2, 16)
            for dst, part, ready in ((w1_hi, w1_half_hi, w1_hi_ready), (w1_lo, w1_half_lo, w1_lo_ready)):
                sp.wait_ge(ready, W1_CHUNKS)
                for half in range(2):
                    for rows in range(2):
                        sp.dma_start(dst[rows * C:(rows + 1) * C, half * E // 2:(half + 1) * E // 2, :].bitcast(F32),
                                     part[half * C:(half + 1) * C, :, :].bitcast(F32)).then_inc(w1_copied, 16)
            for b in range(NB):
                sp.wait_ge(fin_ready, b + 1)
                sp.dma_start(out[b], fin[:, b, :]).then_inc(stored, 16)
            sp.wait_ge(stored, 16 * NB)

        @block.gpsimd
        def _(pool):
            pool.memset(ident[:, :], 0.0).then_inc(pool_const, 1)
            pool.wait_ge(pool_const, 1)
            pool.affine_select(out=ident[:, :], in_=ident[:, :], compare_op=ALU.not_equal, fill=1.0, base=0,
                               pattern=[[-1, P]], channel_multiplier=1).then_inc(pool_const, 1)
            pool.memset(power[:, :], -0.5).then_inc(pool_const, 1)
            pool.iota(pidx[:, :], pattern=[[0, 1]], base=0, channel_multiplier=1).then_inc(pool_const, 1)
            pool.iota(grid[:, :], pattern=[[1, W]], base=0, channel_multiplier=0,
                      allow_small_or_imprecise_dtypes=True).then_inc(pool_const, 1)
            pool.iota(tapyx[:, 0:TAPS], pattern=[[1, KS], [0, KS]], base=-1, channel_multiplier=0,
                      allow_small_or_imprecise_dtypes=True).then_inc(pool_const, 1)
            pool.iota(tapyx[:, TAPS:], pattern=[[0, KS], [1, KS]], base=-1, channel_multiplier=0,
                      allow_small_or_imprecise_dtypes=True).then_inc(pool_const, 1)
            pool.memset(xpad[:, :, :, :].bitcast(F32), 0.0).then_inc(pool_const, 1)

            def rstd(var, src, dst, n, ready):
                pool.wait_ge(var, n)
                pool.wait_ge(pool_const, 3)
                pool.tensor_tensor(dst, src, power[:, 0:src.shape[1]], ALU.pow).then_inc(ready, 1)

            rstd(var1, ve1[:, 0:NT], rs1[:, 0:NT], 1, rstd1)

            pool.memset(sel_f[:, :, :, :], 0.0).then_inc(pool_chain, 1)
            for i, row in enumerate((0, -E)):
                pool.wait_ge(pool_chain, i + 1)
                pool.affine_select(out=sel_f[:, :, :, :], in_=sel_f[:, :, :, :], compare_op=ALU.not_equal, fill=1.0,
                                   base=row, pattern=[[-2, PAIRS], [-1, 2], [0, O]], channel_multiplier=1).then_inc(pool_chain, 1)
            pool.wait_ge(wdcn_hi_ready, 1)
            pool.tensor_tensor(wdcn_lo[:, :, :], wdcn_raw[:, :, :], wdcn_hi[:, :, :].bitcast(F32), ALU.subtract).then_inc(wdcn_ready, 1)
            rstd(var1, ve1[:, NT:], rs1[:, NT:], 2, rstd1)

            def product(u, taps=(0, GROUP)):
                b, g = divmod(u, UNITS)
                if b == 0:
                    pool.wait_ge(hats0_ready[1], 1)
                    if u > 0:
                        pool.wait_ge(hats0_ready[0], 1)
                elif g == 0:
                    pool.wait_ge(haty_ready, b)
                if u >= AT_RING:
                    pool.wait_ge(tap_T, GROUP * (u - AT_RING + 1))
                k0, k1 = (g * GROUP + k for k in taps)
                shape = [P, k1 - k0, H, W]
                for j in range(NT):
                    if on_pool(u, j):
                        last = pool.tensor_tensor(
                            at[:, u % AT_RING, j, taps[0]:taps[1], :].rearrange("p k (y x) -> p k y x", x=W),
                            haty[:, b % 2, j, k0:k1, :].unsqueeze(3).broadcast_to(shape),
                            hats[:, b % 2, j, TAPS + k0:TAPS + k1, :].unsqueeze(2).broadcast_to(shape), ALU.mult)
                        last.then_inc(at_pool, 1)

            pool.wait_ge(pos_ready, 1)
            pool.tensor_tensor(dist[:, 1, :, :], pos[:, 0, 1, 0:2 * TAPS].unsqueeze(2).broadcast_to([P, 2 * TAPS, W]),
                               grid[:, :].unsqueeze(1).broadcast_to([P, 2 * TAPS, W]), ALU.subtract).then_inc(dist_ready, 1)
            pool.wait_ge(mask_ready, 1)
            pool.wait_ge(hats_ready, 1)
            pool.tensor_tensor(haty[:, 0, 1, :, :], hats[:, 0, 1, 0:TAPS, :],
                               mask[:, 0, 1, :].unsqueeze(2).broadcast_to([P, TAPS, H]), ALU.mult).then_inc(hats0_ready[1], 1)
            for k in range(GROUP):
                product(0, (k, k + 1))
            pool.iota(eight[:, :], pattern=[[1, E]], base=0, channel_multiplier=0,
                      allow_small_or_imprecise_dtypes=True).then_inc(eight_ready, 1)

            def distances(b):
                pool.wait_ge(pos_ready, b + 1)
                pool.wait_ge(hats_ready, b)
                pool.tensor_tensor(dist[:, :, :, :],
                                   pos[:, b % 2, :, 0:2 * TAPS].unsqueeze(3).broadcast_to([P, NT, 2 * TAPS, W]),
                                   grid[:, :].unsqueeze(1).unsqueeze(1).broadcast_to([P, NT, 2 * TAPS, W]),
                                   ALU.subtract).then_inc(dist_ready, 1)

            def masked_hats(b):
                pool.wait_ge(tanh_done, b + 1)
                pool.tensor_scalar(mask[:, b % 2, :, :], tanh_m[:, b % 2, :, :], 0.5, 0.5, ALU.mult, ALU.add).then_inc(mask_ready, 1)
                pool.wait_ge(mask_ready, b + 1)
                pool.wait_ge(hats_ready, b + 1)
                pool.tensor_tensor(haty[:, b % 2, :, :, :], hats[:, b % 2, :, 0:TAPS, :],
                                   mask[:, b % 2, :, :].unsqueeze(3).broadcast_to([P, NT, TAPS, H]), ALU.mult).then_inc(haty_ready, 1)

            for beat in range(LAST_BEAT + 1):
                for b in due(beat, POOL_AT["haty"], 1):
                    masked_hats(b)
                for b in due(beat, POOL_AT["dist"], 1):
                    distances(b)
                for u in units_due(beat, POOL_AT["product"]):
                    product(u)
                for i in setup_due(beat, "w1_lo"):
                    if W1_POOL[i]:
                        pool.wait_ge(w1_hi_ready, i + 1)
                        es = slice(i * E // 2 // W1_CHUNKS, (i + 1) * E // 2 // W1_CHUNKS)
                        pool.tensor_tensor(w1_half_lo[:, es, :], w1_raw[:, es, :], w1_half_hi[:, es, :].bitcast(F32), ALU.subtract).then_inc(w1_lo_ready, 1)
                for b in due(beat, POOL_AT["rstd"]):
                    rstd(var2, ve2[:, b % 2, :], rs2[:, b % 2, :], b + 1, rstd2)
                for b, e in second_products(beat):
                    j = e // 2
                    if e % 2 == 1 and 0 < j < PAIRS - (b == NB - 1):
                        pool.wait_ge(tmp_ready, PAIRS * b + j + 1)
                        if j > 1:
                            pool.wait_ge(ya_ready, (PAIRS - 1) * b + j - 1)
                        elif b > 0:
                            pool.wait_ge(fold_done, b)
                        prev = tmp[:, 0, :] if j == 1 else ya[:, j - 2, :]
                        pool.tensor_tensor(ya[:, j - 1, :], prev, tmp[:, j, :], ALU.add).then_inc(ya_ready, 1)

        @block.scalar
        def _(act):
            for half in range(2):
                act.dma_start(woff_raw[half * C:(half + 1) * C, :, :], w_off).then_inc(ld_woff, 16)
            act.wait_ge(pool_const, 3)
            act.activation(tanh_d[:, 0:1], power[:, 0:1], ACT.Gelu).then_inc(act_chain, 1)
            chain = [1]

            def chained(ins):
                chain[0] += 1
                ins.then_inc(act_chain, 1)
                act.wait_ge(act_chain, chain[0])

            def pad_image(b, bank, col):
                act.wait_ge(xn1T, b + 1)
                act.wait_ge(pool_const, CONSTS)
                act.activation(xpad[:, b, 1:1 + H, 1:1 + W],
                               bank[:, col:col + HW].rearrange("p (y x) -> p y x", x=W), ACT.Copy).then_inc(xpad_ready, 1)
                act.activation(xflat[:, b, :], bank[:, col:col + HW], ACT.Copy).then_inc(xflat_ready, 1)

            def save_offsets(b):
                act.wait_ge(om_done, b + 1)
                bank = bank_h[0] if b == 0 else bank_p
                act.activation(om_sb[:, b % 2, :], bank[0:2 * OM, 0:HW], ACT.Copy).then_inc(om_saved, 1)

            def hat_steps(b):
                act.wait_ge(pos_ready, b + 1)
                act.activation(tanh_m[:, b % 2, :, :], pos[:, b % 2, :, 2 * TAPS:], ACT.Tanh, scale=0.5).then_inc(tanh_done, 1)
                act.wait_ge(dist_ready, b + 1)
                first = NT - 1 if b == 0 else 0
                chained(act.activation(adist[:, first:, :, :], dist[:, first:, :, :], ACT.Abs))
                act.activation(hats[:, b % 2, first:, :, :], adist[:, first:, :, :], ACT.Relu, bias=1.0, scale=-1.0).then_inc(hats_ready, 1)

            def value_hi(b, piece):
                st, k0, n = V_PIECES[piece]
                bank = V0_BANKS[piece] if b == 0 else bank_p
                act.wait_ge(v_done, len(V_PIECES) * b + piece + 1)
                act.activation(v_hl[:, b, st, k0:k0 + n, 0:O], bank[:, 0:n * O].rearrange("p (k o) -> p k o", o=O),
                               ACT.Copy).then_inc(v_hi, 1)

            act.wait_ge(ld_wdcn, 32)
            act.activation(wdcn_hi[:, :, :], wdcn_raw[:, :, :], ACT.Copy).then_inc(wdcn_hi_ready, 1)
            pad_image(0, bank_p, 0)
            save_offsets(0)
            hat_steps(0)
            for piece in range(len(V_PIECES)):
                value_hi(0, piece)
            for beat in range(LAST_BEAT + 1):
                for slot in taps_due(beat, ACT_AT["hi"]):
                    act.wait_ge(tap_T, slot + 1)
                    if slot >= A_RING:
                        act.wait_ge(tap_mm, slot - A_RING + 1)
                    act.activation(a_hi[:, slot % A_RING, :, :].rearrange("p s t -> p (s t)"), t_bank(slot)[:, :],
                                   ACT.Copy).then_inc(tap_hi, 1)
                for b in due(beat, ACT_AT["pad"], 1):
                    pad_image(b, bank_p, 0)
                for i in setup_due(beat, "w1_hi"):
                    act.wait_ge(ld_w1, 16)
                    es = slice(i * E // 2 // W1_CHUNKS, (i + 1) * E // 2 // W1_CHUNKS)
                    act.activation(w1_half_hi[:, es, :], w1_raw[:, es, :], ACT.Copy).then_inc(w1_hi_ready, 1)
                if beat == SETUP_AT["sel"]:
                    act.wait_ge(pool_chain, 3)
                    act.activation(sel[:, :, :], sel_f[:, :, :, :].rearrange("r j e o -> r j (e o)"), ACT.Copy).then_inc(sel_ready, 1)
                for b in due(beat, ACT_AT["hats"], 1):
                    hat_steps(b)
                for b in due(beat, ACT_AT["tanh"]):
                    act.wait_ge(diff_ready, b + 1)
                    act.activation(tanh_d[:, :], diff[:, :], ACT.Tanh, scale=0.5).then_inc(tanh_d_done, 1)
                for b in due(beat, ACT_AT["half"]):
                    act.wait_ge(tap_mm, TAPS * (b + 1))
                    if b >= 2:
                        act.wait_ge(t1_ready, b - 1)
                    act.activation(c1[:, b % 2, :], bank_o[O:2 * O, 0:HW], ACT.Copy).then_inc(lo_half, 1)
                for b in due(beat, ACT_AT["conv"], 1):
                    save_offsets(b)
                for b, piece in pieces_due(beat, ACT_AT["value"]):
                    value_hi(b, piece)
                for b in due(beat, ACT_AT["stack"]):
                    act.wait_ge(xn2T, b + 1)
                    if b >= 2:
                        act.wait_ge(h_done, E * (b - 1))
                    act.activation(x2s[:, b % 2, :], bank_c[:, 0:HW], ACT.Copy).then_inc(x2s_ready, 1)
                for b in due(beat, ACT_AT["gate"]):
                    act.wait_ge(lg_done, b + 1)
                    act.activation(lg_sb[:, :], bank_c[0:2 * E, 0:HW], ACT.Copy).then_inc(lg_saved, 1)
                for b in due(beat, ACT_AT["weights"]):
                    act.wait_ge(wdT, b + 1)
                    act.activation(wt[:, :], bank_c[0:2 * E, 0:HW], ACT.Copy).then_inc(wt_ready, 1)
                for half in range(2):
                    for b in due(beat, ACT_AT[f"spread{half}"]):
                        if b == NB - 1:
                            continue
                        act.wait_ge(spread_done, 2 * b + half + 1)
                        if b >= 2:
                            act.wait_ge(tmp_ready, PAIRS * (b - 1))
                        act.activation(spread[:, b % 2, 2 * half:2 * half + 2, :].rearrange("p j t -> p (j t)"),
                                       bank_c[:, :], ACT.Copy).then_inc(spread_ready, 1)
                for b, e in first_products(beat):
                    n = E * b + e
                    act.wait_ge(h_done, n + 1)
                    if n == 0:
                        act.wait_ge(ld_bias, 48)
                    if n >= H_RING:
                        act.wait_ge(y_done, n - H_RING + 1)
                    for c in range(HC):
                        act.activation(hid[:, n % H_RING, c, :], h_bank(n)[:, c * HW:(c + 1) * HW], ACT.Gelu,
                                       bias=b1_col[:, e * HC + c:e * HC + c + 1]).then_inc(h_ready, 1)

        @block.vector
        def _(dve):
            chain = [0]

            def chained(ins):
                chain[0] += 1
                ins.then_inc(dve_chain, 1)
                dve.wait_ge(dve_chain, chain[0])

            def norm_stats(tiles, ready):
                for t in tiles:
                    last = dve.bn_stats(st1[:, t, :], xt[:, t, :])
                chained(last)
                for t in tiles:
                    last = dve.bn_aggr(mv1[:, t, :], st1[:, t, :])
                chained(last)
                a, z = tiles[0], tiles[-1] + 1
                dve.tensor_scalar(ve1[:, a:z], mv1[:, a:z, 1], LN_C_EPS, None, ALU.add).then_inc(ready, 1)

            def norm_apply(tiles, n):
                dve.wait_ge(rstd1, n)
                for t in tiles:
                    last = dve.tensor_scalar(xn1[:, t, :], xt[:, t, :], mv1[:, t, 0:1], rs1[:, t:t + 1], ALU.subtract, ALU.mult)
                chained(last)

            def norm_split(tiles):
                a, z = tiles[0], tiles[-1] + 1
                chained(dve.tensor_copy(xn1_hl[:, a:z, 0:C], xn1[:, a:z, :]))
                dve.tensor_tensor(xn1_hl[:, a:z, C:], xn1[:, a:z, :], xn1_hl[:, a:z, 0:C].bitcast(F32),
                                  ALU.subtract).then_inc(xn1_ready, 1)

            def make_base():
                dve.wait_ge(pool_const, 7)
                dve.tensor_scalar(prow_i[:, :], pidx[:, :], W.bit_length() - 1, None, ALU.arith_shift_right)
                chained(dve.tensor_scalar(pcol_i[:, :], pidx[:, :], W - 1, None, ALU.bitwise_and))
                dve.tensor_copy(prow[:, :], prow_i[:, :])
                chained(dve.tensor_copy(pcol[:, :], pcol_i[:, :]))
                chained(dve.tensor_scalar(tapyx[:, 0:TAPS], tapyx[:, 0:TAPS], prow[:, 0:1], None, ALU.add))
                chained(dve.tensor_scalar(tapyx[:, TAPS:], tapyx[:, TAPS:], pcol[:, 0:1], None, ALU.add))
                for j in range(NT):
                    dve.tensor_scalar(base[:, j, 0:TAPS], tapyx[:, 0:TAPS], float(j * RPT), None, ALU.add)
                    dve.tensor_copy(base[:, j, TAPS:2 * TAPS], tapyx[:, TAPS:])
                    last = dve.memset(base[:, j, 2 * TAPS:], 0.0)
                chained(last)

            def add_bias():
                dve.wait_ge(ld_boff, 16)
                dve.tensor_tensor(base[:, :, :], base[:, :, :], boff_bc[:, :].unsqueeze(1).broadcast_to([P, NT, OM]),
                                  ALU.add).then_inc(base_ready, 1)

            def positions(b):
                dve.wait_ge(omT, b + 1)
                chained(dve.tensor_tensor(pos_a[:, :, :], bank_p[:, 0:NT * 2 * OM].rearrange("p (j m) -> p j m", j=NT)[:, :, 0:OM],
                                          base[:, :, :], ALU.add))
                dve.tensor_tensor(pos[:, b % 2, :, :], bank_p[:, 0:NT * 2 * OM].rearrange("p (j m) -> p j m", j=NT)[:, :, OM:],
                                  pos_a[:, :, :], ALU.add).then_inc(pos_ready, 1)

            def hats_0():
                d, a = dist[:, 0, :, :], adist[:, 0, :, :]
                chained(dve.tensor_tensor(d, pos[:, 0, 0, 0:2 * TAPS].unsqueeze(2).broadcast_to([P, 2 * TAPS, W]),
                                          grid[:, :].unsqueeze(1).broadcast_to([P, 2 * TAPS, W]), ALU.subtract))
                chained(dve.scalar_tensor_tensor(a, d, -1.0, d, ALU.mult, ALU.min))
                dve.tensor_scalar(hats[:, 0, 0, :, :], a, 1.0, 0.0, ALU.add, ALU.max)
                dve.wait_ge(tanh_done, 1)
                dve.tensor_scalar(mask[:, 0, :, :], tanh_m[:, 0, :, :], 0.5, 0.5, ALU.mult, ALU.add).then_inc(mask_ready, 1)
                dve.wait_ge(mask_ready, 1)
                dve.tensor_tensor(haty[:, 0, 0, :, :], hats[:, 0, 0, 0:TAPS, :],
                                  mask[:, 0, 0, :].unsqueeze(2).broadcast_to([P, TAPS, H]), ALU.mult).then_inc(hats0_ready[0], 1)

            def product(slot):
                u = slot // GROUP
                b, k = divmod(slot, TAPS)
                if b == 0:
                    dve.wait_ge(hats0_ready[0], 1)
                    if u > 0:
                        dve.wait_ge(hats0_ready[1], 1)
                elif k == 0:
                    dve.wait_ge(haty_ready, b)
                if u >= AT_RING:
                    dve.wait_ge(tap_T, GROUP * (u - AT_RING + 1))
                for j in range(NT):
                    if not on_pool(u, j):
                        dve.tensor_tensor(
                            at[:, u % AT_RING, j, slot % GROUP, :].rearrange("p (y x) -> p y x", x=W),
                            haty[:, b % 2, j, k, :].unsqueeze(2).broadcast_to([P, H, W]),
                            hats[:, b % 2, j, TAPS + k, :].unsqueeze(1).broadcast_to([P, H, W]), ALU.mult).then_inc(at_dve, 1)

            def value_lo(b, piece):
                st, k0, n = V_PIECES[piece]
                bank = V0_BANKS[piece] if b == 0 else bank_p
                dve.wait_ge(v_hi, len(V_PIECES) * b + piece + 1)
                dve.tensor_tensor(v_hl[:, b, st, k0:k0 + n, O:], bank[:, 0:n * O].rearrange("p (k o) -> p k o", o=O),
                                  v_hl[:, b, st, k0:k0 + n, 0:O].bitcast(F32), ALU.subtract).then_inc(v_lo, 1)

            def split(hi, lo, raw, ready):
                chained(dve.tensor_copy(hi, raw))
                dve.tensor_tensor(lo, raw, hi.bitcast(F32), ALU.subtract).then_inc(ready, 1)

            first, rest = list(range(NT)), list(range(NT, NB * NT))
            make_base()
            dve.wait_ge(ld_xt0, 16)
            norm_stats(first, var1)
            add_bias()
            norm_apply(first, 1)
            norm_split(first)
            dve.wait_ge(ld_woff, 32)
            split(woff[:, :, 0:OM], woff[:, :, OM:], woff_raw[:, :, :], woff_ready)
            dve.wait_ge(ld_xt1, 16)
            norm_stats(rest, var1)
            dve.wait_ge(ld_wg, 32)
            split(wg_hl[:, 0:E], wg_hl[:, E:], wg_raw[:, :], wg_ready)
            dve.tensor_copy(fold[0:O, :], ident[0:O, 0:O])
            dve.tensor_copy(fold[O:, :], ident[O:, O:]).then_inc(fold_ready, 1)
            dve.wait_ge(base_ready, 1)
            positions(0)
            dve.wait_ge(pos_ready, 1)
            hats_0()
            for slot in range(GROUP):
                product(slot)

            def finish(b):
                dve.wait_ge(fold_done, b + 1)
                dve.tensor_tensor(fin[:, b, :], bank_c[0:O, 0:HW], t1[:, b, :], ALU.add).then_inc(fin_ready, 1)

            for beat in range(LAST_BEAT + 1):
                for b in due(beat, DVE_AT["xn"], 1):
                    norm_apply([NT * b, NT * b + 1], 2)
                    norm_split([NT * b, NT * b + 1])
                for b in due(beat, DVE_AT["positions"], 1):
                    positions(b)
                for b, piece in pieces_due(beat, DVE_AT["value"]):
                    value_lo(b, piece)
                for slot in products_due(beat, DVE_AT["product"]):
                    product(slot)
                for slot in taps_due(beat, DVE_AT["lo"]):
                    dve.wait_ge(tap_hi, slot + 1)
                    dve.tensor_tensor(a_lo[:, slot % A_RING, :, :].rearrange("p s t -> p (s t)"), t_bank(slot)[:, :],
                                      a_hi[:, slot % A_RING, :, :].bitcast(F32).rearrange("p s t -> p (s t)"),
                                      ALU.subtract).then_inc(tap_lo, 1)
                for i in setup_due(beat, "w1_lo"):
                    if not W1_POOL[i]:
                        dve.wait_ge(w1_hi_ready, i + 1)
                        es = slice(i * E // 2 // W1_CHUNKS, (i + 1) * E // 2 // W1_CHUNKS)
                        dve.tensor_tensor(w1_half_lo[:, es, :], w1_raw[:, es, :], w1_half_hi[:, es, :].bitcast(F32), ALU.subtract).then_inc(w1_lo_ready, 1)
                for piece in setup_due(beat, "v0_"):
                    value_lo(0, piece)
                for b in due(beat, DVE_AT["residual"]):
                    if b == 0:
                        dve.wait_ge(ld_xc, 16)
                    dve.wait_ge(lo_half, b + 1)
                    chained(dve.tensor_tensor(c2[:, b % 2, :], c1[:, b % 2, :], xc[:, b, :], ALU.add))
                    dve.tensor_tensor(t1[:, b, :], bank_o[0:O, 0:HW], c2[:, b % 2, :], ALU.add).then_inc(t1_ready, 1)
                for b in due(beat, DVE_AT["stats"]):
                    dve.wait_ge(t1T, b + 1)
                    for j in range(NT):
                        last = dve.bn_stats(st2[:, j, :], bank_c[:, j * O:(j + 1) * O])
                    chained(last)
                    for j in range(NT):
                        last = dve.bn_aggr(mv2[:, b % 2, j, :], st2[:, j, :])
                    chained(last)
                    dve.tensor_scalar(ve2[:, b % 2, :], mv2[:, b % 2, :, 1], LN_T_EPS, None, ALU.add).then_inc(var2, 1)
                for b in due(beat, DVE_AT["norm"]):
                    dve.wait_ge(rstd2, b + 1)
                    for j in range(NT):
                        last = dve.tensor_scalar(xn2[:, j, :], bank_c[:, j * O:(j + 1) * O], mv2[:, b % 2, j, 0:1],
                                                 rs2[:, b % 2, j:j + 1], ALU.subtract, ALU.mult)
                    chained(last)
                    if b > 0:
                        dve.wait_ge(xn2T, b)
                    split(xn2_hl[:, :, 0:C], xn2_hl[:, :, C:], xn2[:, :, :], xn2_ready)
                for b in due(beat, DVE_AT["top"]):
                    dve.wait_ge(lgT, b + 1)
                    if b == 0:
                        dve.wait_ge(ld_bias, 48)
                    lg = bank_c[:, 0:NT * 2 * E].rearrange("p (j m) -> p j m", j=NT)
                    chained(dve.tensor_tensor(lg_a[:, :, :], lg[:, :, 0:E],
                                              bg_bc[:, :].unsqueeze(1).broadcast_to([P, NT, E]), ALU.add))
                    dve.tensor_tensor(logit[:, :, :], lg[:, :, E:], lg_a[:, :, :], ALU.add).then_inc(logit_ready, 1)
                    dve.wait_ge(logit_ready, b + 1)
                    for j in range(NT):
                        last = dve.max(top[:, j, :], logit[:, j, :])
                    chained(last)
                    dve.tensor_tensor(diff[:, :], top[:, :, 0], top[:, :, 1], ALU.subtract).then_inc(diff_ready, 1)
                    for j in range(NT):
                        last = dve.max_index(topi[:, j, :], top[:, j, :], logit[:, j, :])
                    chained(last)
                    chained(dve.tensor_copy(topf[:, :, :], topi[:, :, 0:2]))
                    if b == 0:
                        dve.wait_ge(eight_ready, 1)
                    dve.tensor_tensor(onehot[:, :, :, :], eight[:, :].unsqueeze(1).unsqueeze(1).broadcast_to([P, NT, 2, E]),
                                      topf[:, :, :].unsqueeze(3).broadcast_to([P, NT, 2, E]), ALU.is_equal)
                for b in due(beat, DVE_AT["gates"]):
                    dve.wait_ge(tanh_d_done, b + 1)
                    dve.tensor_scalar(pw[:, :, 0], tanh_d[:, :], 0.5, 0.5, ALU.mult, ALU.add)
                    chained(dve.tensor_scalar(pw[:, :, 1], tanh_d[:, :], -0.5, 0.5, ALU.mult, ALU.add))
                    chained(dve.tensor_tensor(gated[:, :, :, :], onehot[:, :, :, :],
                                              pw[:, :, :].unsqueeze(3).broadcast_to([P, NT, 2, E]), ALU.mult))
                    chained(dve.tensor_tensor(wd[:, :, :], gated[:, :, 0, :], gated[:, :, 1, :], ALU.add))
                    split(wd_hl[:, :, 0:E], wd_hl[:, :, E:], wd[:, :, :], wd_ready)
                for half in range(2):
                    for b in due(beat, DVE_AT[f"spread{half}"], NB - 1):
                        dve.wait_ge(spread_done, 2 * b + half + 1)
                        dve.tensor_copy(spread[:, b % 2, 2 * half:2 * half + 2, :].rearrange("p j t -> p (j t)"),
                                        bank_c[:, :]).then_inc(spread_ready, 1)
                for b, e in second_products(beat):
                    if e % 2 == 1:
                        j = e // 2
                        dve.wait_ge(y_done, E * b + e + 1)
                        dve.wait_ge(spread_ready, 2 * b + j // 2 + 1)
                        if b > 0:
                            dve.wait_ge(ya_ready, (PAIRS - 1) * (b - 1) + max(j, 1))
                        dve.scalar_tensor_tensor(tmp[:, j, :], Y_BANKS[b][j][:, 0:HW], b2_col[:, j:j + 1], spread[:, b % 2, j, :],
                                                 ALU.add, ALU.mult).then_inc(tmp_ready, 1)
                for b in due(beat, DVE_AT["fin"]):
                    if b < NB - 1:
                        finish(b)
            finish(NB - 1)

        @block.tensor
        def _(pe):
            released = {}

            def take(name, sem_, value):
                if name in released:
                    pe.wait_ge(*released[name])
                released[name] = (sem_, value)

            def transpose_xn(b, bank, col):
                pe.wait_ge(xn1_ready, b + 1)
                for j in range(NT):
                    last = pe.transpose(bank[:, col + j * P:col + (j + 1) * P], xn1_hl[:, NT * b + j, :].bitcast(F32), ident[:, :])
                last.then_inc(xn1T, 1)

            def conv(b):
                bank = bank_h[0] if b == 0 else bank_p
                if b > 0:
                    take("p", om_saved, b + 1)
                pe.wait_ge(xpad_ready, b + 1)
                for k in range(TAPS):
                    ky, kx = divmod(k, KS)
                    last = pe.matmul(bank[0:2 * OM, 0:HW], woff[:, k, :], xpad[:, b, ky:ky + H, kx:kx + W],
                                     start=(k == 0), stop=(k == TAPS - 1))
                last.then_inc(om_done, 1)

            def transpose_om(b):
                take("p", pos_ready, b + 1)
                for j in range(NT):
                    last = pe.transpose(bank_p[:, j * 2 * OM:(j + 1) * 2 * OM], om_sb[:, b % 2, j * P:(j + 1) * P],
                                        ident[0:2 * OM, 0:2 * OM])
                last.then_inc(omT, 1)

            def value(b, piece):
                st, k0, n = V_PIECES[piece]
                count = len(V_PIECES) * b + piece + 1
                if b == 0:
                    bank = V0_BANKS[piece]
                    released[("c", "y", "o", "h1")[piece]] = (v_lo, count)
                else:
                    bank = bank_p
                    take("p", v_lo, count)
                pe.wait_ge(wdcn_ready, 1)
                pe.wait_ge(xflat_ready, b + 1)
                src = xflat[:, b, st * P:(st + 1) * P]
                pe.matmul(bank[:, 0:n * O], src, wdcn_hi[:, k0:k0 + n, :], start=True, stop=False)
                pe.matmul(bank[:, 0:n * O], src, wdcn_lo[:, k0:k0 + n, :], start=False, stop=True).then_inc(v_done, 1)

            def keep_warm(n, bank):
                for _ in range(n):
                    pe.matmul(bank[:, 0:P], ident[:, :], ident[:, :], start=True, stop=True)

            pe.wait_ge(pool_const, 2)
            keep_warm(WARM, bank_y)
            released["p"] = (xflat_ready, 1)
            transpose_xn(0, bank_p, 0)
            pe.wait_ge(woff_ready, 1)
            conv(0)
            pe.wait_ge(om_saved, 1)
            transpose_om(0)
            for piece in range(len(V_PIECES)):
                value(0, piece)
            keep_warm(WARM_TAPS, bank_t[1])
            def sample(slot):
                b, k = divmod(slot, TAPS)
                pe.wait_ge(tap_lo, slot + 1)
                if k == 0:
                    pe.wait_ge(v_lo, len(V_PIECES) * (b + 1))
                    if b > 0:
                        pe.wait_ge(t1_ready, b)
                for st in range(ST):
                    for part in (a_hi, a_lo):
                        last = pe.matmul(bank_o[:, 0:HW], v_hl[:, b, st, k, :], part[:, slot % A_RING, st, :],
                                         start=(k == 0 and st == 0 and part is a_hi),
                                         stop=(k == TAPS - 1 and st == ST - 1 and part is a_lo))
                last.then_inc(tap_mm, 1)

            def hidden(b, e):
                n = E * b + e
                if n == 0:
                    pe.wait_ge(tap_lo, T_WIDE)
                    pe.wait_ge(w1_copied, 16 * 8)
                if e == 0:
                    pe.wait_ge(x2s_ready, b + 1)
                last_expert = max((m for m in range(n) if h_bank(m) is h_bank(n)), default=None)
                if last_expert is not None:
                    pe.wait_ge(h_ready, HC * (last_expert + 1))
                for c in range(HC):
                    dst = h_bank(n)[:, c * HW:(c + 1) * HW]
                    pe.matmul(dst, w1_hi[:, e, c * P:(c + 1) * P], x2s[:, b % 2, :], start=True, stop=False)
                    last = pe.matmul(dst, w1_lo[:, e, c * P:(c + 1) * P], x2s[:, b % 2, :], start=False, stop=True)
                last.then_inc(h_done, 1)

            def expert_out(n):
                b, e = divmod(n, E)
                j = e // 2
                if n == 0:
                    pe.wait_ge(ld_w2, 16)
                if e % 2 == 0:
                    bank = Y_BANKS[b][j]
                    if bank is bank_y or bank is bank_p:
                        take("y" if bank is bank_y else "p", tmp_ready, PAIRS * b + j + 1)
                    else:
                        pe.wait_ge(tap_lo, SLOTS)
                half = O * (e % 2)
                for c in range(HC):
                    pe.wait_ge(h_ready, HC * n + c + 1)
                    last = pe.matmul(Y_BANKS[b][j][half:half + O, 0:HW], w2_sb[:, e, c, :], hid[:, n % H_RING, c, :],
                                     start=(c == 0), stop=(c == HC - 1))
                last.then_inc(y_done, 1)

            def fold_experts(b):
                take("c", fin_ready, b + 1)
                pe.wait_ge(fold_ready, 1)
                last_b = b == NB - 1
                pe.wait_ge(ya_ready, (PAIRS - 1) * (b + 1) - last_b)
                last = pe.matmul(bank_c[0:O, 0:HW], fold[:, :], ya[:, PAIRS - 2 - last_b, :], start=True, stop=not last_b)
                if last_b:
                    pe.wait_ge(tmp_ready, PAIRS * NB)
                    last = pe.matmul(bank_c[0:O, 0:HW], fold[:, :], tmp[:, PAIRS - 1, :], start=False, stop=True)
                last.then_inc(fold_done, 1)

            pending = []
            for beat in range(LAST_BEAT + 1):
                for slot in taps_due(beat, PE_AT["tap"]):
                    pe.wait_ge(at_dve, made(slot, False))
                    pe.wait_ge(at_pool, made(slot, True))
                    last_tap = max((t for t in range(slot) if t_bank(t) is t_bank(slot)), default=None)
                    if last_tap is not None:
                        pe.wait_ge(tap_lo, last_tap + 1)
                    if slot == 3:
                        pe.wait_ge(v_lo, len(V_PIECES))
                    for st in range(ST):
                        for j in range(NT):
                            last = pe.transpose(t_bank(slot)[:, st * HW + j * P:st * HW + (j + 1) * P],
                                                at[:, slot // GROUP % AT_RING, j, slot % GROUP, st * P:(st + 1) * P], ident[:, :])
                    last.then_inc(tap_T, 1)
                for slot in taps_due(beat, PE_AT["sample"]):
                    sample(slot)
                for b in due(beat, PE_AT["xn"], 1):
                    take("p", xflat_ready, b + 1)
                    transpose_xn(b, bank_p, 0)
                for b in due(beat, PE_AT["conv"], 1):
                    conv(b)
                for b in due(beat, PE_AT["om"], 1):
                    pe.wait_ge(om_saved, b + 1)
                    transpose_om(b)
                for b, piece in pieces_due(beat, PE_AT["value"]):
                    value(b, piece)
                for b in due(beat, PE_AT["t1"]):
                    take("c", xn2_ready, b + 1)
                    pe.wait_ge(t1_ready, b + 1)
                    for j in range(NT):
                        last = pe.transpose(bank_c[:, j * O:(j + 1) * O], t1[:, b, j * P:(j + 1) * P], ident[0:O, 0:O])
                    last.then_inc(t1T, 1)
                for b in due(beat, PE_AT["stack"]):
                    take("c", x2s_ready, b + 1)
                    pe.wait_ge(xn2_ready, b + 1)
                    for j in range(NT):
                        last = pe.transpose(bank_c[:, j * P:(j + 1) * P], xn2_hl[:, j, :].bitcast(F32), ident[:, :])
                    last.then_inc(xn2T, 1)
                for b in due(beat, PE_AT["gate"]):
                    take("c", lg_saved, b + 1)
                    pe.wait_ge(wg_ready, 1)
                    pe.wait_ge(x2s_ready, b + 1)
                    pe.matmul(bank_c[0:2 * E, 0:HW], wg_hl[:, :], x2s[:, b % 2, :], start=True, stop=True).then_inc(lg_done, 1)
                for b in due(beat, PE_AT["logits"]):
                    pe.wait_ge(lg_saved, b + 1)
                    take("c", logit_ready, b + 1)
                    for j in range(NT):
                        last = pe.transpose(bank_c[:, j * 2 * E:(j + 1) * 2 * E], lg_sb[:, j * P:(j + 1) * P], ident[0:2 * E, 0:2 * E])
                    last.then_inc(lgT, 1)
                for b in due(beat, PE_AT["weights"]):
                    take("c", wt_ready, b + 1)
                    pe.wait_ge(wd_ready, b + 1)
                    for j in range(NT):
                        last = pe.transpose(bank_c[0:2 * E, j * P:(j + 1) * P], wd_hl[:, j, :].bitcast(F32), ident[:, :])
                    last.then_inc(wdT, 1)
                for half in range(2):
                    for b in due(beat, PE_AT[f"spread{half}"]):
                        take("c", spread_ready, 2 * b + half + 1)
                        pe.wait_ge(wt_ready, b + 1)
                        pe.wait_ge(sel_ready, 1)
                        for j in range(2):
                            last = pe.matmul(bank_c[:, j * HW:(j + 1) * HW], sel[:, 2 * half + j, :], wt[:, :], start=True, stop=True)
                        last.then_inc(spread_done, 1)
                for b, e in first_products(beat):
                    hidden(b, e)
                    pending.append(E * b + e)
                    if len(pending) > LAG:
                        expert_out(pending.pop(0))
                for b in due(beat, PE_AT["fold"]):
                    if b < NB - 1:
                        fold_experts(b)
            while pending:
                expert_out(pending.pop(0))
            fold_experts(NB - 1)


def kernel(**inputs):
    import numpy as np
    import concourse.bacc as bacc
    from concourse.bass_utils import run_bass_kernel_spmd

    x = np.asarray(inputs["x"])
    w_off = np.asarray(inputs["L0_conv_w_off"])
    b_off = np.asarray(inputs["L0_conv_b_off"])
    order = np.concatenate([np.arange(TAPS) * 2, np.arange(TAPS) * 2 + 1, np.arange(2 * TAPS, 3 * TAPS)])
    arrays = {
        "x_tok": x.reshape(NB, C, NT, P).transpose(3, 0, 2, 1).reshape(P, NB * NT, C),
        "x_ch": x.reshape(NB, C, HW).transpose(1, 0, 2),
        "w_off": w_off[order].reshape(OM, C, TAPS).transpose(1, 2, 0),
        "b_off": b_off[order],
        "w_dcn": np.asarray(inputs["L0_conv_w_dcn"]).reshape(O, C, TAPS).transpose(1, 2, 0),
        "wg": np.asarray(inputs["L0_ffn_Wg"]),
        "bg": np.asarray(inputs["L0_ffn_bg"]),
        "w1": np.asarray(inputs["L0_ffn_W1"]).reshape(2, E // 2, C, HID).transpose(0, 2, 1, 3).reshape(P, E // 2, HID),
        "b1": np.asarray(inputs["L0_ffn_b1"]).reshape(E * HC, P).T,
        "w2": np.asarray(inputs["L0_ffn_W2"]).reshape(E, HC, P, O).transpose(2, 0, 1, 3),
        "b2": np.asarray(inputs["L0_ffn_b2"]).reshape(PAIRS, 2 * O).T,
    }
    arrays = {f"in_{n}": np.ascontiguousarray(a) for n, a in arrays.items()}
    nc = bacc.Bacc("TRN2", target_bir_lowering=False, num_devices=1)
    args = [nc.dram_tensor(n, a.shape, mybir.dt.from_np(a.dtype), kind="ExternalInput").ap() for n, a in arrays.items()]
    out = nc.dram_tensor("out_0", (NB, C, HW), F32, kind="ExternalOutput").ap()
    metaformer_kernel(nc, *args, out)
    r = run_bass_kernel_spmd(nc, [arrays], core_ids=[0])
    return r.results[0]["out_0"].reshape(NB, C, H, W)
```
